# Optimizing a Trainium2 kernel written in Bass

```python
import numpy as np
import jax
import jax.numpy as jnp

def _softmax(x, axis=-1):
    return jax.nn.softmax(x, axis=axis)

def _gelu(x):
    return jax.nn.gelu(x, approximate=True)

def _silu(x):
    return jax.nn.silu(x)

def _sigmoid(x):
    return jax.nn.sigmoid(x)

def _layernorm(x, axis=-1, eps=1e-05):
    m = jnp.mean(x, axis=axis, keepdims=True)
    v = jnp.var(x, axis=axis, keepdims=True)
    return (x - m) / jnp.sqrt(v + eps)

def _scatter_add(tgt, idx, src, axis=0):
    return tgt.at[idx].add(src)

def _segment_sum(src, seg, n):
    return jax.ops.segment_sum(src, seg, n)
kernel_name = 'mk_metaformer_d1_conv_nhwc768_r2_efc742'

def setup_inputs(seed: int=0):
    np.random.seed(seed)
    _w = jnp.asarray

    def _rec_inputs():
        import jax
        import jax.numpy as jnp
        _gk = jax.random.key(seed)
        x = -0.0005963 + 1.001 * jax.random.normal(jax.random.fold_in(_gk, 1), (1, 32, 32, 384), jnp.float32)
        return x
    x = _rec_inputs()

    def _L0_conv_setup():
        import jax, jax.numpy as jnp
        import numpy as np
        DIM = 384
        NUM_HEADS = 12
        HEAD_DIM = DIM // NUM_HEADS
        H = W = 32

        def get_rel_pos(q_size, k_size, rel_pos):
            coords = jnp.arange(q_size)[:, None] - jnp.arange(k_size)[None, :] + (k_size - 1)
            return rel_pos[coords]

        def add_decomposed_rel_pos(attn, q, rel_pos_h, rel_pos_w, q_size, k_size):
            q_h, q_w = q_size
            k_h, k_w = k_size
            Rh = get_rel_pos(q_h, k_h, rel_pos_h)
            Rw = get_rel_pos(q_w, k_w, rel_pos_w)
            Bn, _, c = q.shape
            r_q = q.reshape(Bn, q_h, q_w, c)
            rel_h = jnp.einsum('bhwc,hkc->bhwk', r_q, Rh)
            rel_w = jnp.einsum('bhwc,wkc->bhwk', r_q, Rw)
            attn = attn.reshape(Bn, q_h, q_w, k_h, k_w)
            attn = attn + rel_h[..., :, None] + rel_w[..., None, :]
            return attn.reshape(Bn, q_h * q_w, k_h * k_w)
        key = jax.random.key(seed)
        ks = jax.random.split(key, 7)
        inv = 1.0 / np.sqrt(DIM)
        return {'x': jax.random.normal(ks[0], (1, H, W, DIM), jnp.float32), 'w_qkv': jax.random.normal(ks[1], (DIM, 3 * DIM), jnp.float32) * inv, 'b_qkv': jax.random.normal(ks[2], (3 * DIM,), jnp.float32) * 0.02, 'w_proj': jax.random.normal(ks[3], (DIM, DIM), jnp.float32) * inv, 'b_proj': jax.random.normal(ks[4], (DIM,), jnp.float32) * 0.02, 'rel_pos_h': jax.random.normal(ks[5], (2 * H - 1, HEAD_DIM), jnp.float32) * 0.02, 'rel_pos_w': jax.random.normal(ks[6], (2 * W - 1, HEAD_DIM), jnp.float32) * 0.02}
    _L0_conv_all = _L0_conv_setup()
    _L0_conv_in = {k: v for k, v in _L0_conv_all.items() if k in ('w_qkv', 'b_qkv', 'w_proj', 'b_proj', 'rel_pos_h', 'rel_pos_w')}
    del _L0_conv_all

    def _L0_ffn_setup():
        import jax, jax.numpy as jnp
        import numpy as np
        NUM_EXPERTS = 8
        TOP_K = 2
        CAPACITY_FACTOR = 1.25
        MAX_GROUP_SIZE = 2048
        MIN_EXPERT_CAPACITY = 4

        def _moe_forward(x, w_router, wi, wo):
            B, T, D = x.shape
            E = NUM_EXPERTS
            num_tokens = B * T
            G = max(num_tokens // MAX_GROUP_SIZE, E)
            while num_tokens % G != 0 or G % E != 0:
                G += 1
            S = num_tokens // G
            C = max(int(TOP_K * CAPACITY_FACTOR * S / E), MIN_EXPERT_CAPACITY)
            xg = x.reshape(G, S, D)
            logits = jnp.einsum('gsd,de->gse', xg.astype(jnp.float32), w_router.astype(jnp.float32))
            probs = jax.nn.softmax(logits, axis=-1)
            gate, idx = jax.lax.top_k(probs, TOP_K)
            idx_kf = jnp.swapaxes(idx, 1, 2).reshape(G, TOP_K * S)
            mask = jax.nn.one_hot(idx_kf, E, dtype=jnp.int32)
            prio = jnp.cumsum(mask, axis=1) * mask - 1
            prio = jnp.swapaxes(prio.reshape(G, TOP_K, S, E), 1, 2)
            prio_se = prio.max(axis=2)
            gate_se = jnp.einsum('gsk,gske->gse', gate, jax.nn.one_hot(idx, E, dtype=gate.dtype))
            dispatch = jax.nn.one_hot(prio_se, C, dtype=x.dtype)
            combine = dispatch * gate_se[..., None].astype(x.dtype)
            expert_in = jnp.einsum('gsec,gsd->egcd', dispatch, xg)
            h = jax.nn.relu(jnp.einsum('egcd,edf->egcf', expert_in, wi))
            expert_out = jnp.einsum('egcf,efd->egcd', h, wo)
            out = jnp.einsum('gsec,egcd->gsd', combine, expert_out)
            return out.reshape(B, T, D)
        key = jax.random.key(seed)
        k1, k2, k3, k4 = jax.random.split(key, 4)
        B, T, D, F = (8, 512, 384, 1536)
        x = jax.random.normal(k1, (B, T, D), jnp.float32)
        w_router = jax.random.normal(k2, (D, NUM_EXPERTS), jnp.float32) * D ** (-0.5)
        wi = jax.random.normal(k3, (NUM_EXPERTS, D, F), jnp.float32) * D ** (-0.5)
        wo = jax.random.normal(k4, (NUM_EXPERTS, F, D), jnp.float32) * F ** (-0.5)
        return {'x': x, 'w_router': w_router, 'wi': wi, 'wo': wo}
    _L0_ffn_all = _L0_ffn_setup()
    _L0_ffn_in = {k: v for k, v in _L0_ffn_all.items() if k in ('w_router', 'wi', 'wo')}
    del _L0_ffn_all
    return {'x': x, 'L0_conv_w_qkv': _L0_conv_in['w_qkv'], 'L0_conv_b_qkv': _L0_conv_in['b_qkv'], 'L0_conv_w_proj': _L0_conv_in['w_proj'], 'L0_conv_b_proj': _L0_conv_in['b_proj'], 'L0_conv_rel_pos_h': _L0_conv_in['rel_pos_h'], 'L0_conv_rel_pos_w': _L0_conv_in['rel_pos_w'], 'L0_ffn_w_router': _L0_ffn_in['w_router'], 'L0_ffn_wi': _L0_ffn_in['wi'], 'L0_ffn_wo': _L0_ffn_in['wo']}

def reference(x, L0_conv_w_qkv, L0_conv_b_qkv, L0_conv_w_proj, L0_conv_b_proj, L0_conv_rel_pos_h, L0_conv_rel_pos_w, L0_ffn_w_router, L0_ffn_wi, L0_ffn_wo):
    import jax
    import jax.numpy as jnp

    def _L0_conv_ref(x, w_qkv, b_qkv, w_proj, b_proj, rel_pos_h, rel_pos_w):
        import jax, jax.numpy as jnp
        import numpy as np
        DIM = 384
        NUM_HEADS = 12
        HEAD_DIM = DIM // NUM_HEADS
        H = W = 32

        def get_rel_pos(q_size, k_size, rel_pos):
            coords = jnp.arange(q_size)[:, None] - jnp.arange(k_size)[None, :] + (k_size - 1)
            return rel_pos[coords]

        def add_decomposed_rel_pos(attn, q, rel_pos_h, rel_pos_w, q_size, k_size):
            q_h, q_w = q_size
            k_h, k_w = k_size
            Rh = get_rel_pos(q_h, k_h, rel_pos_h)
            Rw = get_rel_pos(q_w, k_w, rel_pos_w)
            Bn, _, c = q.shape
            r_q = q.reshape(Bn, q_h, q_w, c)
            rel_h = jnp.einsum('bhwc,hkc->bhwk', r_q, Rh)
            rel_w = jnp.einsum('bhwc,wkc->bhwk', r_q, Rw)
            attn = attn.reshape(Bn, q_h, q_w, k_h, k_w)
            attn = attn + rel_h[..., :, None] + rel_w[..., None, :]
            return attn.reshape(Bn, q_h * q_w, k_h * k_w)
        B, h, w, _ = x.shape
        N = h * w
        scale = HEAD_DIM ** (-0.5)
        qkv = x @ w_qkv + b_qkv
        qkv = qkv.reshape(B, N, 3, NUM_HEADS, HEAD_DIM)
        qkv = jnp.transpose(qkv, (2, 0, 3, 1, 4)).reshape(3, B * NUM_HEADS, N, HEAD_DIM)
        q, k, v = (qkv[0], qkv[1], qkv[2])
        attn = jnp.einsum('bnd,bmd->bnm', q * scale, k)
        attn = add_decomposed_rel_pos(attn, q, rel_pos_h, rel_pos_w, (h, w), (h, w))
        attn = jax.nn.softmax(attn.astype(jnp.float32), axis=-1).astype(q.dtype)
        out = attn @ v
        out = out.reshape(B, NUM_HEADS, h, w, HEAD_DIM)
        out = jnp.transpose(out, (0, 2, 3, 1, 4)).reshape(B, h, w, DIM)
        return out @ w_proj + b_proj

    def _L0_ffn_ref(x, w_router, wi, wo):
        import jax, jax.numpy as jnp
        import numpy as np
        NUM_EXPERTS = 8
        TOP_K = 2
        CAPACITY_FACTOR = 1.25
        MAX_GROUP_SIZE = 2048
        MIN_EXPERT_CAPACITY = 4

        def _moe_forward(x, w_router, wi, wo):
            B, T, D = x.shape
            E = NUM_EXPERTS
            num_tokens = B * T
            G = max(num_tokens // MAX_GROUP_SIZE, E)
            while num_tokens % G != 0 or G % E != 0:
                G += 1
            S = num_tokens // G
            C = max(int(TOP_K * CAPACITY_FACTOR * S / E), MIN_EXPERT_CAPACITY)
            xg = x.reshape(G, S, D)
            logits = jnp.einsum('gsd,de->gse', xg.astype(jnp.float32), w_router.astype(jnp.float32))
            probs = jax.nn.softmax(logits, axis=-1)
            gate, idx = jax.lax.top_k(probs, TOP_K)
            idx_kf = jnp.swapaxes(idx, 1, 2).reshape(G, TOP_K * S)
            mask = jax.nn.one_hot(idx_kf, E, dtype=jnp.int32)
            prio = jnp.cumsum(mask, axis=1) * mask - 1
            prio = jnp.swapaxes(prio.reshape(G, TOP_K, S, E), 1, 2)
            prio_se = prio.max(axis=2)
            gate_se = jnp.einsum('gsk,gske->gse', gate, jax.nn.one_hot(idx, E, dtype=gate.dtype))
            dispatch = jax.nn.one_hot(prio_se, C, dtype=x.dtype)
            combine = dispatch * gate_se[..., None].astype(x.dtype)
            expert_in = jnp.einsum('gsec,gsd->egcd', dispatch, xg)
            h = jax.nn.relu(jnp.einsum('egcd,edf->egcf', expert_in, wi))
            expert_out = jnp.einsum('egcf,efd->egcd', h, wo)
            out = jnp.einsum('gsec,egcd->gsd', combine, expert_out)
            return out.reshape(B, T, D)
        return _moe_forward(x, w_router, wi, wo)

    def _gn(v, G=32, eps=1e-05):
        B_, H_, W_, C_ = v.shape
        g = v.reshape(B_, H_, W_, G, C_ // G)
        m = jnp.mean(g, axis=(1, 2, 4), keepdims=True)
        s = jnp.var(g, axis=(1, 2, 4), keepdims=True)
        return ((g - m) / jnp.sqrt(s + eps)).reshape(v.shape)

    def _ln_c(v, eps=1e-06):
        m = jnp.mean(v, axis=-1, keepdims=True)
        s = jnp.var(v, axis=-1, keepdims=True)
        return (v - m) / jnp.sqrt(s + eps)

    def _ln_t(v, eps=1e-05):
        m = jnp.mean(v, axis=-1, keepdims=True)
        s = jnp.var(v, axis=-1, keepdims=True)
        return (v - m) / jnp.sqrt(s + eps)

    def _to_tokens(v):
        B_, H_, W_, C_ = v.shape
        return v.reshape(B_, H_ * W_, C_)

    def _from_tokens(t, like):
        return t.reshape(like.shape)
    x = x + _L0_conv_ref(_ln_c(x), L0_conv_w_qkv, L0_conv_b_qkv, L0_conv_w_proj, L0_conv_b_proj, L0_conv_rel_pos_h, L0_conv_rel_pos_w)
    t = _to_tokens(x)
    t = t + _L0_ffn_ref(_ln_t(t), L0_ffn_w_router, L0_ffn_wi, L0_ffn_wo)
    x = _from_tokens(t, x)
    return x

_drawn_inputs = setup_inputs


def setup_inputs(seed=0):
    import zlib

    import numpy as np

    out = dict(_drawn_inputs(seed))
    spreads = {}
    factors = {'L0_conv_rel_pos_h': 4.484, 'L0_conv_rel_pos_w': 4.485}
    for name, (base, spread) in spreads.items():
        noise = np.random.default_rng([zlib.crc32(name.encode()), seed]).standard_normal(out[name].shape)
        drawn = base * np.exp(spread * noise) if base else spread * noise
        out[name] = jnp.asarray(drawn.astype(out[name].dtype))
    for name, factor in factors.items():
        out[name] = (out[name] * factor).astype(out[name].dtype)
    return out
```

```python
from contextlib import ExitStack

import concourse.bass as bass
from concourse import mybir

ALU = mybir.AluOpType
ACT = mybir.ActivationFunctionType
AX_X = mybir.AxisListType.X
F32 = mybir.dt.float32
F32R = mybir.dt.float32r
U32 = mybir.dt.uint32

P = 128
BANK = 512
SIDE = 32
LN_C_EPS = 1e-6
LN_T_EPS = 1e-5


def metaformer_layer(nc, x, w_qkv, b_qkv, w_proj, b_proj, rel_pos_h, rel_pos_w, w_router, wi, wo,
                     ident_c, flip_c, onehot_c, tri_c, slot_c, out):
    T, D = SIDE * SIDE, x.shape[3]
    NT, DC = T // P, D // P
    HD = rel_pos_h.shape[1]
    NH = D // HD
    HPG = P // HD
    NREL = rel_pos_h.shape[0]
    E, _, F = wi.shape
    C = max(int(2 * 1.25 * P / E), 4)
    SLOTS = NT * C
    SCALE = float(HD) ** -0.5
    UF = 3
    UNITS = F // (UF * P)
    PAIRS = E // 2
    PU = 2 * UNITS
    RG = P // C
    ROW_TILES = [(g, min(RG, NT - g)) for g in range(0, NT, RG)]
    NR = len(ROW_TILES)
    PS = 2 * C
    assert T == 8 * P and HD == 32 and NH == 12 and E == 8 and NT == 8 and UNITS * UF * P == F

    x_v = x.rearrange("a h w d -> (a h w) d").rearrange("(t p) d -> p t d", p=P)
    out_v = out.rearrange("a h w d -> (a h w) d").rearrange("(t p) d -> p t d", p=P)
    wi_v = wi.rearrange("e (c p) (s f) -> e s p c f", p=P, s=UNITS)
    wo_v = wo.rearrange("e (s k p) d -> e s p k d", p=P, s=UNITS)

    at = [(nc.sbuf_base + 63) // 64 * 64]

    def room(nbytes):
        here = at[0]
        at[0] += (nbytes + 31) // 32 * 32
        return here

    def place(name, shape, dt, offset):
        return nc.alloc_sbuf_tensor_at(name, shape, dt, offset=offset)

    def new(name, shape, dt=F32):
        n = 4
        for s in shape[1:]:
            n *= s
        return place(name, shape, dt, room(n))

    TD = 4 * NT * D
    xs = new("xs", [P, NT, D])
    ident = new("ident", [P, P])
    ones = new("ones", [P, P])
    tri = new("tri", [P, P])
    slot1 = new("slot1", [P, C])
    flip = new("flip", [NREL, NREL])
    bqk = new("bqk", [P, 2 * DC])
    wrt = new("wrt", [P, DC, E])
    stats = new("stats", [P, NT, 6])
    mv = new("mv", [P, NT, 2])
    veps = new("veps", [P, NT])
    std = new("std", [P, NT])
    rstd = new("rstd", [P, NT])
    gsl = new("gsl", [PS, PAIRS * NT])
    gsc = new("gsc", [PS, NT])
    base = at[0]

    u1, u2 = room(TD), room(TD)
    xn = place("xn", [P, NT, D], F32, u1)
    qf = place("qf", [P, DC, T], F32, u1)
    attn = place("attn", [P, NT, D], F32, u1)
    xnT = place("xnT", [P, DC, T], F32, u2)
    onehot = place("onehot", [P, T], F32, u2)
    rst = place("rst", [P, 2, BANK], F32, u2)
    attnT = place("attnT", [P, DC, T], F32, u2)
    u3 = room(4 * DC * 3 * D)
    wqkv = place("wqkv", [P, DC, 3 * D], F32, u3)
    prob = place("prob", [P, 2, T], F32, u3)
    wpj = new("wpj", [P, DC, D])
    b4 = room(4 * D)
    bv = place("bv", [P, D], F32, b4)
    mneg = place("mneg", [NT, 2, P], F32R, b4)
    rl = place("rl", [P, 2, 2, NT // 2], F32, b4 + 4 * 2 * P)
    bpj = new("bpj", [P, D])
    qh, ql, kh, kl = (new(n, [P, DC, T], F32R) for n in ("qh", "ql", "kh", "kl"))
    rel_hi = [new(n, [P, DC, T], F32R) for n in ("rhh", "rwh")]
    rel_lo = [new(n, [P, DC, T], F32R) for n in ("rhl", "rwl")]
    vt = new("vt", [P, NT, D])
    aq, bq, ak, bk = ([new(f"{n}{b}", [P, T], F32R) for b in range(2)] for n in ("aq", "bq", "ak", "bk"))
    vh = [new(f"vh{b}", [P, NT, 2 * HD]) for b in range(2)]
    o4 = room(4 * 2 * BANK)
    osb = place("osb", [P, 2, BANK], F32, o4)
    bd = place("bd", [P, 2, HPG, NREL], F32, o4)
    rmax = new("rmax", [P, 2, NT])
    rp = place("rp", [NREL, 2, HPG, HD], F32, o4 + 4 * BANK)
    b6 = place("b6", [2 * DC, P], F32, o4 + 6 * BANK)
    top = at[0]

    at[0] = base
    e1, e2, e3 = room(TD), room(TD), room(2 * TD)
    tn = place("tn", [P, NT, D], F32, e1)
    dg = place("dg", [P, NT, E, C], F32, e1)
    tnT = place("tnT", [P, DC, T], F32, e2)
    hh = place("hh", [P, 2, UF, SLOTS], F32R, e1)
    hl = place("hl", [P, 2, UF, SLOTS], F32R, e1 + 4 * 2 * UF * SLOTS)
    th = place("th", [P, NT, D], F32R, e3)
    tl = place("tl", [P, NT, D], F32R, e3 + TD)
    eo = place("eo", [P, NR, D], F32, e3)
    comb = place("comb", [PS, NT, D], F32, e3 + 4 * NR * D)
    ch = place("ch", [PS, 2, D], F32R, e3 + 4 * NR * D + TD)
    cl = place("cl", [PS, 2, D], F32R, e3 + 4 * NR * D + TD + 8 * D)
    assert 4 * NR * D + TD + 16 * D <= 2 * TD and 16 * UF * SLOTS <= 2 * TD
    dsp = new("dsp", [P, NT, E, C], F32R)
    dpt = new("dpt", [PS, PAIRS, NT, P], F32R)
    dpc = new("dpc", [PS, NT, P], F32R)
    xeh, xel = (new(n, [P, DC, E, SLOTS], F32R) for n in ("xeh", "xel"))
    raw_i = new("raw_i", [P, 2, DC, UF * P])
    raw_o = new("raw_o", [P, 2, UF, D])
    wih, wil = (new(n, [P, 2, DC, UF * P], F32R) for n in ("wih", "wil"))
    woh, wol = (new(n, [P, 2, UF, D], F32R) for n in ("woh", "wol"))
    end, at[0] = at[0], at[0] - 8 * UF * D
    lg, ex, pr, mk1, mk2, gate, cm1, cm2, pos = (
        new(n, [P, NT, E]) for n in ("lg", "ex", "pr", "mk1", "mk2", "gate", "cm1", "cm2", "pos"))
    top8 = new("top8", [P, NT, 8])
    idx8 = new("idx8", [P, NT, 8], U32)
    idxf = new("idxf", [P, NT, 2])
    lmax, lsum, lrec = (new(n, [P, NT]) for n in ("lmax", "lsum", "lrec"))
    assert at[0] <= end and max(top, end) <= nc.sbuf_usable_end

    ctx = ExitStack()
    with ctx:
        ps = ctx.enter_context(nc.psum_tensor("ps", [P, 8 * BANK], F32))

        def bank(i, n=BANK):
            return ps[:, i * BANK:i * BANK + n]

        def sem(name):
            return ctx.enter_context(nc.semaphore(name))

        def wait(eng, s, value):
            if not isinstance(value, int) or value > 0:
                eng.wait_ge(s, value)

        x_in = [sem("x_in0"), sem("x_in1")]
        small_in, wqkv_in, wpj_in = sem("small_in"), sem("wqkv_in"), sem("wpj_in")
        raw_i_in = [sem("raw_i_in0"), sem("raw_i_in1")]
        raw_o_in = [sem("raw_o_in0"), sem("raw_o_in1")]
        ln_step, ln_var, ln_std = sem("ln_step"), sem("ln_var"), sem("ln_std")
        xn_ready, ones_set, bd_zero, rp_turned, bd_ready = (
            sem(n) for n in ("xn_ready", "ones_set", "bd_zero", "rp_turned", "bd_ready"))
        xb_ready, k_rows = sem("xb_ready"), sem("k_rows")
        turned, turn_act, turn_dve = sem("turned"), sem("turn_act"), sem("turn_dve")
        proj_mm, q_act, hi_act, lo_dve, v_dve = (sem(n) for n in ("proj_mm", "q_act", "hi_act", "lo_dve", "v_dve"))
        rel_products_mm, rel_copied, rel_mm, rel_act, rel_dve = (
            sem(n) for n in ("rel_products_mm", "rel_copied", "rel_mm", "rel_act", "rel_dve"))
        heads_in = [sem("heads_in0"), sem("heads_in1")]
        vh_ready, max_mm, max_red, max_turned, mneg_ready = (
            sem(n) for n in ("vh_ready", "max_mm", "max_red", "max_turned", "mneg_ready"))
        mrow_in = [sem("mrow_in0"), sem("mrow_in1")]
        s_mm, exp_done, pv_mm, o_copied, o_turned, o_rec, o_normed = (
            sem(n) for n in ("s_mm", "exp_done", "pv_mm", "o_copied", "o_turned", "o_rec", "o_normed"))
        wproj_mm, x1_ready = sem("wproj_mm"), sem("x1_ready")
        th_ready, tl_ready, logits_mm, rt_step, ex_ready, masks_ready, count_mm = (
            sem(n) for n in ("th_ready", "tl_ready", "logits_mm", "rt_step", "ex_ready", "masks_ready", "count_mm"))
        dsp_ready, dg_ready, gsl_mm, gsl_ready = (
            sem(n) for n in ("dsp_ready", "dg_ready", "gsl_mm", "gsl_ready"))
        dpt_mm, dpt_act, dpt_dve, xe_mm, xe_act, xe_dve = (
            sem(n) for n in ("dpt_mm", "dpt_act", "dpt_dve", "xe_mm", "xe_act", "xe_dve"))
        wi_hi, wi_lo, wo_hi, wo_lo = (sem(n) for n in ("wi_hi", "wi_lo", "wo_hi", "wo_lo"))
        h_mm, h_hi, h_lo, y_mm, eo_ready, eo_moved = (
            sem(n) for n in ("h_mm", "h_hi", "h_lo", "y_mm", "eo_ready", "eo_moved"))
        pair_set, c_hi, c_lo, c_mm, c_added, out_done = (
            sem(n) for n in ("pair_set", "c_hi", "c_lo", "c_mm", "c_added", "out_done"))

        block = ctx.enter_context(nc.Block())

        SMALL = [
            (flip[:, :], flip_c), (rp[:, 0, :, :], rel_pos_h.unsqueeze(1).broadcast_to([NREL, HPG, HD])),
            (rp[:, 1, :, :], rel_pos_w.unsqueeze(1).broadcast_to([NREL, HPG, HD])),
            (ident[:, :], ident_c), (b6[:, :], b_qkv[0:2 * D].rearrange("(m p) -> m p", p=P)),
            (bv[:, :], b_qkv[2 * D:3 * D].partition_broadcast(P)), (bpj[:, :], b_proj.partition_broadcast(P)),
            (tri[:, :], tri_c), (slot1[:, :], slot_c), (wrt[:, :, :], w_router.rearrange("(c p) e -> p c e", p=P)),
            (onehot[2 * SIDE:4 * SIDE, :], onehot_c),
        ]
        SMALL_IN = 16 * len(SMALL)
        HALF = NT // 2
        HEAD_IN = 16 * 10

        def rel_views(rel, n):
            kind, c, half = n // (2 * DC), n // 2 % DC, n % 2
            b, w = bank(2 + n % 6), SIDE // 2
            if kind == 0:
                return rel[kind][:, c, half * BANK:(half + 1) * BANK], b
            return (rel[kind][:, c, :].rearrange("p (r w) -> p w r", w=SIDE)[:, half * w:(half + 1) * w, :],
                    b.rearrange("p (w r) -> p w r", w=w))

        @block.sync
        def _(sp):
            for n in range(2):
                sp.dma_start(xs[:, n * HALF:(n + 1) * HALF, :], x_v[:, n * HALF:(n + 1) * HALF, :]).then_inc(x_in[n], 16)
            for dst, src in SMALL:
                sp.dma_start(dst, src).then_inc(small_in, 16)
            sp.dma_start(wqkv[:, :, :], w_qkv.rearrange("(c p) n -> p c n", p=P)).then_inc(wqkv_in, 16)
            sp.dma_start(wpj[:, :, :], w_proj.rearrange("(c p) n -> p c n", p=P)).then_inc(wpj_in, 16)

            def gather_head(chunk, j, h):
                b, rows = j % 2, slice(HD * j, HD * (j + 1))
                wait(sp, s_mm, 8 * (h - 1))
                sp.wait_ge(rel_dve, 4 * DC)
                parts = [(aq[b], 0, qh), (aq[b], 1, ql), (aq[b], 2, rel_hi[0]), (aq[b], 3, rel_hi[1]),
                         (bq[b], 0, qh), (bq[b], 1, rel_lo[0]), (bq[b], 2, rel_lo[1]),
                         (ak[b], 0, kh), (ak[b], 1, kh), (bk[b], 0, kl)]
                for dst, n, src in parts:
                    sp.dma_start(dst[HD * n:HD * (n + 1), :].bitcast(F32), src[rows, chunk, :].bitcast(F32)).then_inc(heads_in[b], 16)

            def max_row(b, h):
                sp.wait_ge(mneg_ready, h + 1)
                sp.dma_start(bq[b][3 * HD:3 * HD + 1, :].rearrange("o (t q) -> o t q", q=P).bitcast(F32),
                             mneg[:, b, :].bitcast(F32)).then_inc(mrow_in[b], 16)

            sp.wait_ge(hi_act, 4 * DC)
            sp.wait_ge(lo_dve, 4 * DC)
            sp.wait_ge(rel_act, 4 * DC)
            sp.wait_ge(rel_dve, 4 * DC)
            gather_head(0, 0, 0)
            for j in range(1, HPG):
                gather_head(0, j, j)
                max_row((j - 1) % 2, j - 1)
            with sp.Fori(1, DC) as g:
                for j in range(HPG):
                    gather_head(g, j, g * HPG + j)
                    max_row((j + 1) % 2, g * HPG + j - 1)
            max_row((NH - 1) % 2, NH - 1)

            def load_unit(e, s, u):
                b = s % 2
                wait(sp, wi_lo, u - 1)
                sp.wait_ge(x1_ready, NT)
                sp.dma_start(raw_i[:, b, :, :], wi_v[e, s]).then_inc(raw_i_in[b], 16)
                wait(sp, wo_lo, u - 1)
                sp.wait_ge(x1_ready, NT)
                sp.dma_start(raw_o[:, b, :, :], wo_v[e, s]).then_inc(raw_o_in[b], 16)

            def move_output(k, pr):
                sp.wait_ge(eo_ready, NR * (2 * pr + k + 1))
                for g in range(NT):
                    sp.dma_start(comb[C * k:C * (k + 1), g, :],
                                 eo[C * (g % RG):C * (g % RG + 1), g // RG, :]).then_inc(eo_moved, 16)

            for u in range(PU):
                load_unit(u // UNITS, u % UNITS, u)
            with sp.Fori(0, PAIRS - 1) as pr:
                for k in range(2):
                    move_output(k, pr)
                    for s in range(UNITS):
                        load_unit(2 * pr + 2 + k, s, PU * pr + PU + UNITS * k + s)
            for k in range(2):
                move_output(k, PAIRS - 1)

            for t in range(NT):
                sp.wait_ge(c_added, NT * (PAIRS - 1) + t + 1)
                sp.dma_start(out_v[:, t, :], xs[:, t, :]).then_inc(out_done, 16)
            sp.wait_ge(out_done, 16 * NT)

        @block.gpsimd
        def _(pool):
            nc.gpsimd.memset(ones[:, :], 1.0).then_inc(ones_set, 1)
            for b in range(2):
                nc.gpsimd.memset(vh[b][:, :, HD:2 * HD], 1.0).then_inc(ones_set, 1)
            pool.wait_ge(xn_ready, NT)
            for t in range(NT):
                nc.gpsimd.tensor_tensor(xs[:, t, :], xs[:, t, :], bpj[:, :], ALU.add).then_inc(xb_ready, 1)
            pool.wait_ge(v_dve, NT)

            def head_values(h, b):
                wait(pool, pv_mm, 8 * (h - 1))
                nc.gpsimd.tensor_copy(vh[b][:, :, 0:HD], vt[:, :, bass.ts(h, HD)]).then_inc(vh_ready, 1)

            head_values(0, 0)
            head_values(1, 1)
            with pool.Fori(1, NH // 2) as i:
                for b in range(2):
                    head_values(2 * i + b, b)

            def set_pair(pr):
                wait(pool, c_mm, NT * pr)
                wait(pool, c_lo, NT * pr)
                nc.gpsimd.tensor_copy(dpc[:, :, :], dpt[:, pr, :, :].bitcast(F32)).then_inc(pair_set, 1)
                nc.gpsimd.tensor_copy(gsc[:, :], gsl[:, bass.ts(pr, NT)]).then_inc(pair_set, 1)

            pool.wait_ge(dpt_act, PAIRS)
            pool.wait_ge(dpt_dve, PAIRS)
            pool.wait_ge(gsl_ready, 1)
            set_pair(0)
            with pool.Fori(1, PAIRS) as pr:
                set_pair(pr)

        @block.tensor
        def _(pe):
            mm = nc.tensor.matmul

            pe.wait_ge(small_in, SMALL_IN)
            for kind in range(2):
                nc.tensor.transpose(bank(6)[:, NREL * kind:NREL * (kind + 1)],
                                    rp[:, kind, :, :].rearrange("p a b -> p (a b)"), flip[:, :]).then_inc(rp_turned, 1)
            nc.tensor.transpose(bank(6)[:, 2 * NREL:2 * NREL + 2 * DC], b6[:, :],
                                ident[0:2 * DC, 0:2 * DC]).then_inc(rp_turned, 1)

            def turn(src, ready, done):
                for half in range(2):
                    if ready is not None:
                        pe.wait_ge(*ready(half))
                    for c in range(DC):
                        for t in range(HALF):
                            last = nc.tensor.transpose(bank(half * DC + c)[:, t * P:(t + 1) * P],
                                                       src[:, half * HALF + t, c * P:(c + 1) * P], ident[:, :])
                        last.then_inc(turned, 1)

            turn(xn, lambda half: (xn_ready, HALF * (half + 1)), turned)

            pe.wait_ge(turn_act, DC)
            pe.wait_ge(turn_dve, DC)
            pe.wait_ge(bd_ready, 2)
            pe.wait_ge(wqkv_in, 16)
            seq = 0

            def free(n):
                if n < 0:
                    return
                if n < 6:
                    pe.wait_ge(q_act, n + 1)
                elif n < 12:
                    pe.wait_ge(lo_dve, n + 1)
                else:
                    pe.wait_ge(v_dve, n - 11)

            for m in range(2 * DC):
                for half in range(2):
                    free(seq - 8)
                    for c in range(DC):
                        last = mm(bank((6 + seq) % 8), wqkv[:, c, m * P:(m + 1) * P],
                                  xnT[:, c, half * BANK:(half + 1) * BANK], start=c == 0, stop=c == DC - 1)
                    last.then_inc(proj_mm, 1)
                    seq += 1
            for t in range(NT):
                free(seq - 8)
                for c in range(DC):
                    last = mm(bank((6 + seq) % 8, D), xnT[:, c, t * P:(t + 1) * P], wqkv[:, c, 2 * D:3 * D],
                              start=c == 0, stop=c == DC - 1)
                last.then_inc(proj_mm, 1)
                seq += 1

            def rel_products(n):
                kind, c, half = n // (2 * DC), n // 2 % DC, n % 2
                wait(pe, rel_copied, n - 1)
                for t in range(HALF):
                    for j in range(HPG):
                        r = (half * HALF + t) * HPG + j
                        q_of_r = qf[:, c, r * SIDE:(r + 1) * SIDE] if kind == 0 else qf[:, c, r:T:SIDE]
                        last = mm(bank(n % 2)[j * SIDE:(j + 1) * SIDE, t * P:(t + 1) * P], q_of_r,
                                  bd[:, kind, :, SIDE - 1 - r:2 * SIDE - 1 - r], start=True, stop=True)
                last.then_inc(rel_products_mm, 1)

            def rel_turn(n):
                pe.wait_ge(rel_copied, n + 1)
                wait(pe, rel_dve, n - 5)
                for t in range(HALF):
                    last = nc.tensor.transpose(bank(2 + n % 6)[:, t * P:(t + 1) * P],
                                               rst[:, n % 2, t * P:(t + 1) * P], ident[:, :])
                last.then_inc(rel_mm, 1)

            pe.wait_ge(q_act, 2 * DC)
            pe.wait_ge(lo_dve, 4 * DC)
            pe.wait_ge(v_dve, NT)
            for n in range(4 * DC):
                rel_products(n)
                if n > 0:
                    rel_turn(n - 1)
            rel_turn(4 * DC - 1)
            pe.wait_ge(rel_dve, 4 * DC)
            pe.wait_ge(k_rows, 8)

            def max_scores(h, n, b, t):
                if t == 0:
                    pe.wait_ge(heads_in[b], HEAD_IN * (n + 1))
                wait(pe, max_red, 8 * h + t)
                for half in range(2):
                    last = mm(bank(4 + half), aq[b][:, t * P:(t + 1) * P], ak[b][:, half * BANK:(half + 1) * BANK],
                              start=True, stop=True)
                last.then_inc(max_mm, 1)

            def turn_max(h, b):
                pe.wait_ge(max_red, 8 * h + 8)
                wait(pe, o_normed, h - 1)
                nc.tensor.transpose(bank(7)[0:NT, 0:P], rmax[:, b, :], ident[:, :]).then_inc(max_turned, 1)

            def scores(h, n, b, t):
                if t == 0:
                    pe.wait_ge(mrow_in[b], 16 * (n + 1))
                wait(pe, exp_done, 8 * h + t - 1)
                for half in range(2):
                    cols = slice(half * BANK, (half + 1) * BANK)
                    mm(bank(2 * (t % 2) + half), ak[b][:, t * P:(t + 1) * P], aq[b][:, cols], start=True, stop=False)
                    last = mm(bank(2 * (t % 2) + half), bk[b][0:3 * HD + 1, t * P:(t + 1) * P],
                              bq[b][0:3 * HD + 1, cols], start=False, stop=True)
                last.then_inc(s_mm, 1)

            def values(h, b, t):
                pe.wait_ge(exp_done, 8 * h + t + 1)
                if t == 0:
                    pe.wait_ge(vh_ready, h + 1)
                    wait(pe, o_copied, h)
                for half in range(2):
                    last = mm(bank(6)[2 * HD * half:2 * HD * (half + 1), :], vh[b][:, t, :],
                              prob[:, t % 2, half * BANK:(half + 1) * BANK], start=t == 0, stop=t == NT - 1)
                last.then_inc(pv_mm, 1)

            def turn_output(h, b):
                pe.wait_ge(o_copied, h + 1)
                wait(pe, mneg_ready, MN(h))
                for j in range(HALF):
                    last = nc.tensor.transpose(bank(7)[:, j * P:(j + 1) * P], osb[:, b, j * P:(j + 1) * P], ident[:, :])
                last.then_inc(o_turned, 1)

            def MN(h):
                return h + 2 if not isinstance(h, int) else min(h + 2, NH)

            def head(h, n, b, first=False, last=False):
                o = 1 - b
                nn = n + b
                for t in range(NT):
                    nxt = not last and 3 <= t < 7
                    if t == 7 and not last:
                        turn_max(h + 1, o)
                    if t == 2 and not first:
                        turn_output(h - 1, o)
                    if nxt:
                        max_scores(h + 1, nn, o, 2 * (t - 3))
                    scores(h, n, b, t)
                    if nxt:
                        max_scores(h + 1, nn, o, 2 * (t - 3) + 1)
                    if t > 0:
                        values(h, b, t - 1)
                    elif not first:
                        values(h - 1, o, NT - 1)

            for t in range(NT):
                max_scores(0, 0, 0, t)
            turn_max(0, 0)
            head(0, 0, 0, first=True)
            with pe.Fori(0, (NH - 2) // 2) as i:
                head(2 * i + 1, i, 1)
                head(2 * i + 2, i + 1, 0)
            head(NH - 1, (NH - 1) // 2, 1, last=True)
            values(NH - 1, 1, NT - 1)
            pe.wait_ge(o_normed, NH - 1)
            turn_output(NH - 1, 1)

            pe.wait_ge(exp_done, 8 * NH)
            pe.wait_ge(o_normed, NH)
            turn(attn, None, turned)
            pe.wait_ge(turn_act, 2 * DC)
            pe.wait_ge(turn_dve, 2 * DC)
            pe.wait_ge(wpj_in, 16)
            for t in range(NT):
                for c in range(DC):
                    last = mm(bank((6 + t) % 8, D), attnT[:, c, t * P:(t + 1) * P], wpj[:, c, :],
                              start=c == 0, stop=c == DC - 1)
                last.then_inc(wproj_mm, 1)

            turn(tn, lambda half: (xn_ready, NT + HALF * (half + 1)), turned)
            pe.wait_ge(turn_act, 3 * DC)
            pe.wait_ge(turn_dve, 3 * DC)
            for g in range(NT):
                for c in range(DC):
                    last = mm(bank(6)[:, g * E:(g + 1) * E], tnT[:, c, g * P:(g + 1) * P], wrt[:, c, :],
                              start=c == 0, stop=c == DC - 1)
            last.then_inc(logits_mm, 1)
            pe.wait_ge(masks_ready, 2)
            first_choice = mk1[:, :, :].rearrange("p g e -> p (g e)")
            second_choice = mk2[:, :, :].rearrange("p g e -> p (g e)")
            W = NT * E
            mm(bank(7, W), tri[:, :], first_choice, start=True, stop=True).then_inc(count_mm, 1)
            mm(bank(5, W), tri[:, :], second_choice, start=True, stop=False)
            mm(bank(5, W), ones[:, :], first_choice, start=False, stop=True).then_inc(count_mm, 1)

            pe.wait_ge(dsp_ready, 1)
            pe.wait_ge(th_ready, NT)
            pe.wait_ge(tl_ready, NT)
            n = 0
            for g in range(NT):
                slots = dsp[:, g, :, :].rearrange("p e c -> p (e c)")
                for c in range(DC):
                    for part in (th, tl):
                        if n >= 8:
                            pe.wait_ge((xe_act, xe_dve)[n % 2], n // 2 - 3)
                        mm(bank(n % 8, E * C), part[:, g, c * P:(c + 1) * P], slots,
                           start=True, stop=True).then_inc(xe_mm, 1)
                        n += 1
            n = 0
            pe.wait_ge(xe_act, NT * DC)
            pe.wait_ge(xe_dve, NT * DC)
            for pr in range(PAIRS):
                for half in range(2):
                    for q in range(HALF):
                        g = half * HALF + q
                        last = nc.tensor.transpose(
                            bank(n)[0:PS, q * P:(q + 1) * P],
                            dsp[:, g, 2 * pr:2 * pr + 2, :].rearrange("p e c -> p (e c)").bitcast(F32), ident[:, :])
                    last.then_inc(dpt_mm, 1)
                    n += 1
            pe.wait_ge(dg_ready, 1)
            pe.wait_ge(dpt_act, 1)
            for pr in range(PAIRS):
                for g in range(NT):
                    k = pr * NT + g
                    last = mm(bank(0)[0:PS, k:k + 1], dg[:, g, 2 * pr:2 * pr + 2, :].rearrange("p e c -> p (e c)"),
                              ones[:, 0:1], start=True, stop=True)
            last.then_inc(gsl_mm, 1)
            pe.wait_ge(gsl_ready, 1)
            pe.wait_ge(dpt_act, PAIRS)
            pe.wait_ge(dpt_dve, PAIRS)

            def hidden(e, b, v):
                pe.wait_ge(wi_hi, v + 1)
                pe.wait_ge(wi_lo, v + 1)
                for k in range(UF):
                    wait(pe, h_lo, UF * (v - 1) + k + 1)
                    terms = [(wih, xeh), (wih, xel), (wil, xeh)]
                    for c in range(DC):
                        for n, (w, xe) in enumerate(terms):
                            last = mm(bank(k, SLOTS), w[:, b, c, k * P:(k + 1) * P], xe[:, c, e, :],
                                      start=c == 0 and n == 0, stop=c == DC - 1 and n == 2)
                    last.then_inc(h_mm, 1)

            def output(s, e, v):
                b = s % 2
                pe.wait_ge(wo_hi, v + 1)
                pe.wait_ge(wo_lo, v + 1)
                if s == 0:
                    wait(pe, eo_ready, NR * e)
                for k in range(UF):
                    pe.wait_ge(h_lo, UF * v + k + 1)
                    for r, (g0, gn) in enumerate(ROW_TILES):
                        rows = slice(g0 * C, (g0 + gn) * C)
                        for n, (h, w) in enumerate([(hh, woh), (hl, woh), (hh, wol)]):
                            last = mm(bank(3 + r, D)[0:gn * C, :], h[:, b, k, rows], w[:, b, k, :],
                                      start=s == 0 and k == 0 and n == 0,
                                      stop=s == UNITS - 1 and k == UF - 1 and n == 2)
                last.then_inc(y_mm, 1)

            def combine(pr):
                pe.wait_ge(pair_set, 2 * pr + 2)
                for g in range(NT):
                    pe.wait_ge(c_lo, NT * pr + g + 1)
                    if g >= 2:
                        pe.wait_ge(c_added, NT * pr + g - 1)
                    mm(bank(6 + g % 2, D), dpc[:, g, :], ch[:, g % 2, :], start=True, stop=False)
                    mm(bank(6 + g % 2, D), dpc[:, g, :], cl[:, g % 2, :], start=False, stop=True).then_inc(c_mm, 1)

            def pair(pr, first=False, last=False):
                for k in range(PU):
                    v = PU * pr + k
                    if not (last and k == PU - 1):
                        hidden(2 * pr + (k + 1) // UNITS, (k + 1) % 2, v + 1)
                    output(k % UNITS, 2 * pr + k // UNITS, v)
                    if k == 1 and not first:
                        combine(pr - 1)

            hidden(0, 0, 0)
            pair(0, first=True)
            with pe.Fori(1, PAIRS - 1) as pr:
                pair(pr)
            pair(PAIRS - 1, last=True)
            combine(PAIRS - 1)

        @block.scalar
        def _(act):
            run = nc.scalar.activation

            def turn_back(dst, n):
                for k in range(0, 2 * DC, 2):
                    act.wait_ge(turned, 2 * DC * n + k + 1)
                    run(dst[:, k % DC, (k // DC) * BANK:(k // DC + 1) * BANK], bank(k), ACT.Copy).then_inc(turn_act, 1)

            act.wait_ge(ones_set, 3)
            act.wait_ge(small_in, SMALL_IN)
            for b in range(2):
                run(ak[b][2 * SIDE:4 * SIDE, :], onehot[2 * SIDE:4 * SIDE, :], ACT.Copy).then_inc(k_rows, 1)
                for n in range(2):
                    run(bk[b][HD * (n + 1):HD * (n + 2), :], onehot[SIDE * (n + 2):SIDE * (n + 3), :],
                        ACT.Copy).then_inc(k_rows, 1)
                run(bk[b][3 * HD:3 * HD + 1, :], ones[3 * HD:3 * HD + 1, 0:1].broadcast_to([1, T]),
                    ACT.Copy).then_inc(k_rows, 1)
            act.wait_ge(ln_var, 1)
            run(std[:, :], veps[:, :], ACT.Sqrt).then_inc(ln_std, 1)
            act.wait_ge(k_rows, 8)
            turn_back(xnT, 0)
            act.wait_ge(bd_ready, 2)
            seq = 0
            for m in range(DC):
                for half in range(2):
                    cols = slice(half * BANK, (half + 1) * BANK)
                    act.wait_ge(proj_mm, seq + 1)
                    run(qf[:, m, cols], bank((6 + seq) % 8), ACT.Identity, bias=bqk[:, m:m + 1]).then_inc(q_act, 1)
                    act.wait_ge(q_act, seq + 1)
                    run(qh[:, m, cols], qf[:, m, cols], ACT.Copy, scale=SCALE).then_inc(hi_act, 1)
                    seq += 1
            for m in range(DC):
                for half in range(2):
                    act.wait_ge(proj_mm, seq + 1)
                    run(kh[:, m, half * BANK:(half + 1) * BANK], bank((6 + seq) % 8), ACT.Identity,
                        bias=bqk[:, DC + m:DC + m + 1]).then_inc(hi_act, 1)
                    seq += 1

            def rel_high(n):
                act.wait_ge(rel_mm, n + 1)
                dst, src = rel_views(rel_hi, n)
                run(dst, src, ACT.Copy).then_inc(rel_act, 1)

            for n in range(4 * DC):
                act.wait_ge(rel_products_mm, n + 1)
                wait(act, rel_mm, n - 1)
                run(rst[:, n % 2, :], bank(n % 2), ACT.Copy).then_inc(rel_copied, 1)
                if n > 0:
                    rel_high(n - 1)
            rel_high(4 * DC - 1)

            def exps(h, b, first=False):
                for t in range(NT):
                    act.wait_ge(s_mm, 8 * h + t + 1)
                    wait(act, pv_mm, 8 * h + t - 1)
                    run(prob[:, t % 2, :], ps[:, 2 * (t % 2) * BANK:2 * (t % 2 + 1) * BANK], ACT.Exp).then_inc(exp_done, 1)
                    if t == 0 and not first:
                        copy_output(h - 1, 1 - b)

            def copy_output(h, b):
                act.wait_ge(pv_mm, 8 * h + 8)
                run(osb[:, b, :], bank(6), ACT.Copy).then_inc(o_copied, 1)

            exps(0, 0, first=True)
            with act.Fori(0, (NH - 2) // 2) as i:
                exps(2 * i + 1, 1)
                exps(2 * i + 2, 0)
            exps(NH - 1, 1)
            copy_output(NH - 1, 1)
            turn_back(attnT, 1)

            act.wait_ge(ln_var, 2)
            run(std[:, :], veps[:, :], ACT.Sqrt).then_inc(ln_std, 1)
            for t in range(NT):
                act.wait_ge(xn_ready, NT + t + 1)
                run(th[:, t, :], tn[:, t, :], ACT.Copy).then_inc(th_ready, 1)
            turn_back(tnT, 2)
            act.wait_ge(rt_step, 2)
            run(ex[:, :, :], lg[:, :, :], ACT.Exp).then_inc(ex_ready, 1)
            n = 0
            for g in range(NT):
                for c in range(DC):
                    act.wait_ge(xe_mm, n + 1)
                    run(xeh[:, c, :, g * C:(g + 1) * C],
                        bank(n % 8, E * C).rearrange("p (e c) -> p e c", e=E), ACT.Copy).then_inc(xe_act, 1)
                    n += 2
            for pr in range(PAIRS):
                act.wait_ge(dpt_mm, 2 * pr + 1)
                run(dpt[:, pr, 0:HALF, :].rearrange("p g s -> p (g s)"), bank(2 * pr)[0:PS, :], ACT.Copy).then_inc(dpt_act, 1)

            def split_wi(b, v, n):
                act.wait_ge(raw_i_in[b], 16 * (n + 1))
                wait(act, h_mm, UF * (v - 1))
                run(wih[:, b, :, :], raw_i[:, b, :, :], ACT.Copy).then_inc(wi_hi, 1)

            def split_wo(b, v, n):
                act.wait_ge(raw_o_in[b], 16 * (n + 1))
                wait(act, y_mm, v - 1)
                run(woh[:, b, :, :], raw_o[:, b, :, :], ACT.Copy).then_inc(wo_hi, 1)

            def relu(b, v):
                wait(act, y_mm, v - 1)
                for k in range(UF):
                    act.wait_ge(h_mm, UF * v + k + 1)
                    run(hh[:, b, k, :], bank(k, SLOTS), ACT.Relu).then_inc(h_hi, 1)

            def leave(e):
                act.wait_ge(y_mm, UNITS * (e + 1))
                wait(act, eo_moved, 16 * NT * e)
                for r, (g0, gn) in enumerate(ROW_TILES):
                    run(eo[0:gn * C, r, :], bank(3 + r, D)[0:gn * C, :], ACT.Copy).then_inc(eo_ready, 1)

            def gated(pr):
                act.wait_ge(eo_moved, 16 * NT * (2 * pr + 2))
                act.wait_ge(pair_set, 2 * pr + 2)
                for g in range(NT):
                    if g >= 2:
                        act.wait_ge(c_mm, NT * pr + g - 1)
                    run(ch[:, g % 2, :], comb[:, g, :], ACT.Copy, scale=gsc[:, g:g + 1]).then_inc(c_hi, 1)

            def pair(pr, first=False, last=False):
                for k in range(PU):
                    v = PU * pr + k
                    relu(k % 2, v)
                    if k == 0 and not first:
                        leave(2 * pr - 1)
                    if k == UNITS:
                        leave(2 * pr)
                    if k == 2 and not first:
                        gated(pr - 1)
                    if not (last and k + 2 >= PU):
                        split_wi(k % 2, v + 2, PU // 2 * pr + k // 2 + 1)
                    if not (last and k + 1 >= PU):
                        split_wo((k + 1) % 2, v + 1, PU // 2 * pr + (k + 1) // 2)

            split_wi(0, 0, 0)
            split_wi(1, 1, 0)
            split_wo(0, 0, 0)
            pair(0, first=True)
            with act.Fori(1, PAIRS - 1) as pr:
                pair(pr)
            pair(PAIRS - 1, last=True)
            leave(E - 1)
            gated(PAIRS - 1)

        @block.vector
        def _(dve):
            ve = nc.vector
            stt = ve.scalar_tensor_tensor

            def norm(src, dst, eps, n, ready):
                s0 = n * 3 * NT
                for t in range(NT):
                    ready(t)
                    ve.bn_stats(stats[:, t, :], src[:, t, :]).then_inc(ln_step, 1)
                dve.wait_ge(ln_step, s0 + NT)
                for t in range(NT):
                    ve.bn_aggr(mv[:, t, :], stats[:, t, :]).then_inc(ln_step, 1)
                dve.wait_ge(ln_step, s0 + 2 * NT)
                ve.tensor_scalar(veps[:, :], mv[:, :, 1], eps, None, ALU.add).then_inc(ln_var, 1)
                dve.wait_ge(ln_std, n + 1)
                ve.reciprocal(rstd[:, :], std[:, :]).then_inc(ln_step, NT)
                dve.wait_ge(ln_step, s0 + 3 * NT)
                for t in range(NT):
                    ve.tensor_scalar(dst[:, t, :], src[:, t, :], mv[:, t, 0:1], rstd[:, t:t + 1],
                                     ALU.subtract, ALU.mult).then_inc(xn_ready, 1)

            def turn_back(dst, n):
                for k in range(1, 2 * DC, 2):
                    dve.wait_ge(turned, 2 * DC * n + k + 1)
                    ve.tensor_copy(dst[:, k % DC, (k // DC) * BANK:(k // DC + 1) * BANK], bank(k)).then_inc(turn_dve, 1)

            ve.memset(bd[:, :, :, :], 0.0).then_inc(bd_zero, 1)
            norm(xs, xn, LN_C_EPS, 0, lambda t: dve.wait_ge(x_in[t // HALF], 16))
            dve.wait_ge(bd_zero, 1)
            dve.wait_ge(rp_turned, 3)
            ve.tensor_copy(bqk[:, :], bank(6)[:, 2 * NREL:2 * NREL + 2 * DC]).then_inc(bd_ready, 1)
            for j in range(HPG):
                rows = slice(HD * j, HD * (j + 1))
                last = ve.tensor_copy(bd[rows, :, j, :], bank(6, 2 * NREL)[rows, :].rearrange("p (k r) -> p k r", k=2))
            last.then_inc(bd_ready, 1)
            dve.wait_ge(k_rows, 8)
            turn_back(xnT, 0)
            seq = 0
            for m in range(DC):
                for half in range(2):
                    cols = slice(half * BANK, (half + 1) * BANK)
                    dve.wait_ge(hi_act, seq + 1)
                    stt(out=ql[:, m, cols], in0=qf[:, m, cols], scalar=SCALE, in1=qh[:, m, cols].bitcast(F32),
                        op0=ALU.mult, op1=ALU.subtract).then_inc(lo_dve, 1)
                    seq += 1
            for m in range(DC):
                for half in range(2):
                    cols = slice(half * BANK, (half + 1) * BANK)
                    dve.wait_ge(hi_act, seq + 1)
                    stt(out=kl[:, m, cols], in0=bank((6 + seq) % 8), scalar=bqk[:, DC + m:DC + m + 1],
                        in1=kh[:, m, cols].bitcast(F32), op0=ALU.add, op1=ALU.subtract).then_inc(lo_dve, 1)
                    seq += 1
            for t in range(NT):
                dve.wait_ge(proj_mm, seq + 1)
                ve.tensor_tensor(vt[:, t, :], bank((6 + seq) % 8, D), bv[:, :], ALU.add).then_inc(v_dve, 1)
                seq += 1
            for n in range(4 * DC):
                dve.wait_ge(rel_act, n + 1)
                dst, src = rel_views(rel_lo, n)
                ve.tensor_tensor(dst, src, rel_views(rel_hi, n)[0].bitcast(F32), ALU.subtract).then_inc(rel_dve, 1)

            def reduce_max(h, b, t):
                dve.wait_ge(max_mm, 8 * h + t + 1)
                ve.tensor_reduce(rmax[:, b, t:t + 1], ps[:, 4 * BANK:6 * BANK], AX_X, ALU.max).then_inc(max_red, 1)

            def negate_max(h, b):
                dve.wait_ge(max_turned, h + 1)
                ve.tensor_scalar(mneg[:, b, :], bank(7)[0:NT, 0:P], -1.0, None, ALU.mult).then_inc(mneg_ready, 1)

            def normalise(h, b):
                turned_o = bank(7).rearrange("p (j s c) -> p s j c", s=2, c=2 * HD)
                dve.wait_ge(o_turned, h + 1)
                ve.reciprocal(rl[:, b, :, :], turned_o[:, :, :, HD]).then_inc(o_rec, 1)
                dve.wait_ge(o_rec, h + 1)
                ve.tensor_tensor(attn[:, :, bass.ts(h, HD)].rearrange("p (s j) d -> p s j d", s=2),
                                 turned_o[:, :, :, 0:HD],
                                 rl[:, b, :, :].unsqueeze(3).broadcast_to([P, 2, HALF, HD]), ALU.mult).then_inc(o_normed, 1)

            def head(h, b, first=False, last=False):
                if not first:
                    normalise(h - 1, 1 - b)
                if not last:
                    for t in range(NT):
                        reduce_max(h + 1, 1 - b, t)
                    negate_max(h + 1, 1 - b)

            for t in range(NT):
                reduce_max(0, 0, t)
            negate_max(0, 0)
            head(0, 0, first=True)
            with dve.Fori(0, (NH - 2) // 2) as i:
                head(2 * i + 1, 1)
                head(2 * i + 2, 0)
            head(NH - 1, 1, last=True)
            normalise(NH - 1, 1)
            turn_back(attnT, 1)

            dve.wait_ge(xb_ready, NT)
            for t in range(NT):
                dve.wait_ge(wproj_mm, t + 1)
                ve.tensor_tensor(xs[:, t, :], bank((6 + t) % 8, D), xs[:, t, :], ALU.add).then_inc(x1_ready, 1)
            norm(xs, tn, LN_T_EPS, 1, lambda t: dve.wait_ge(x1_ready, t + 1))
            for t in range(NT):
                dve.wait_ge(th_ready, t + 1)
                ve.tensor_tensor(tl[:, t, :], tn[:, t, :], th[:, t, :].bitcast(F32), ALU.subtract).then_inc(tl_ready, 1)
            turn_back(tnT, 2)

            steps = [0]

            def step(ins):
                steps[0] += 1
                ins.then_inc(rt_step, 1)
                dve.wait_ge(rt_step, steps[0])

            def over(v, n):
                return v.unsqueeze(len(v.shape)).broadcast_to([*v.shape, n])

            logits = bank(6, NT * E).rearrange("p (g e) -> p g e", e=E)
            dve.wait_ge(logits_mm, 1)
            step(ve.tensor_reduce(lmax[:, :], logits, AX_X, ALU.max))
            step(ve.tensor_tensor(lg[:, :, :], logits, over(lmax[:, :], E), ALU.subtract))
            dve.wait_ge(ex_ready, 1)
            step(ve.tensor_reduce(lsum[:, :], ex[:, :, :], AX_X, ALU.add))
            step(ve.reciprocal(lrec[:, :], lsum[:, :]))
            step(ve.tensor_tensor(pr[:, :, :], ex[:, :, :], over(lrec[:, :], E), ALU.mult))
            for g in range(NT):
                last = ve.max(top8[:, g, :], pr[:, g, :])
                if g < NT - 1:
                    last.then_inc(rt_step, 1)
                    steps[0] += 1
            step(last)
            for g in range(NT):
                last = ve.max_index(idx8[:, g, :], top8[:, g, :], pr[:, g, :])
                if g < NT - 1:
                    last.then_inc(rt_step, 1)
                    steps[0] += 1
            step(last)
            step(ve.tensor_copy(idxf[:, :, :], idx8[:, :, 0:2]))
            step(ve.tensor_scalar(idxf[:, :, :], idxf[:, :, :], 1.0, None, ALU.add))
            number = slot1[:, 0:E].unsqueeze(1).broadcast_to([P, NT, E])
            ve.tensor_tensor(mk1[:, :, :], number, idxf[:, :, 0:1].broadcast_to([P, NT, E]), ALU.is_equal).then_inc(masks_ready, 1)
            ve.tensor_tensor(mk2[:, :, :], number, idxf[:, :, 1:2].broadcast_to([P, NT, E]), ALU.is_equal).then_inc(masks_ready, 1)
            dve.wait_ge(masks_ready, 2)
            step(ve.tensor_tensor(gate[:, :, :], mk1[:, :, :], top8[:, :, 0:1].broadcast_to([P, NT, E]), ALU.mult))
            step(ve.tensor_tensor(cm1[:, :, :], mk2[:, :, :], top8[:, :, 1:2].broadcast_to([P, NT, E]), ALU.mult))
            step(ve.tensor_tensor(gate[:, :, :], gate[:, :, :], cm1[:, :, :], ALU.add))
            dve.wait_ge(count_mm, 2)
            step(ve.tensor_tensor(cm1[:, :, :], bank(7, NT * E).rearrange("p (g e) -> p g e", e=E), mk1[:, :, :], ALU.mult))
            step(ve.tensor_tensor(cm2[:, :, :], bank(5, NT * E).rearrange("p (g e) -> p g e", e=E), mk2[:, :, :], ALU.mult))
            step(ve.tensor_tensor(pos[:, :, :], cm1[:, :, :], cm2[:, :, :], ALU.add))
            ge = [P, NT * E, C]
            ve.tensor_tensor(dsp[:, :, :, :].rearrange("p g e c -> p (g e) c"), slot1[:, :].unsqueeze(1).broadcast_to(ge),
                             over(pos[:, :, :].rearrange("p g e -> p (g e)"), C), ALU.is_equal).then_inc(dsp_ready, 1)
            dve.wait_ge(dsp_ready, 1)
            dve.wait_ge(turned, 6 * DC)
            ve.tensor_tensor(dg[:, :, :, :].rearrange("p g e c -> p (g e) c"),
                             dsp[:, :, :, :].rearrange("p g e c -> p (g e) c").bitcast(F32),
                             over(gate[:, :, :].rearrange("p g e -> p (g e)"), C), ALU.mult).then_inc(dg_ready, 1)
            n = 1
            for g in range(NT):
                for c in range(DC):
                    dve.wait_ge(xe_mm, n + 1)
                    ve.tensor_copy(xel[:, c, :, g * C:(g + 1) * C],
                                   bank(n % 8, E * C).rearrange("p (e c) -> p e c", e=E)).then_inc(xe_dve, 1)
                    n += 2
            for q in range(PAIRS):
                dve.wait_ge(dpt_mm, 2 * q + 2)
                ve.tensor_copy(dpt[:, q, HALF:NT, :].rearrange("p g s -> p (g s)"), bank(2 * q + 1)[0:PS, :]).then_inc(dpt_dve, 1)
            dve.wait_ge(gsl_mm, 1)
            ve.tensor_copy(gsl[:, :], bank(0)[0:PS, 0:PAIRS * NT]).then_inc(gsl_ready, 1)

            def split_wi(b, v):
                dve.wait_ge(wi_hi, v + 1)
                ve.tensor_tensor(wil[:, b, :, :], raw_i[:, b, :, :], wih[:, b, :, :].bitcast(F32),
                                 ALU.subtract).then_inc(wi_lo, 1)

            def split_wo(b, v):
                dve.wait_ge(wo_hi, v + 1)
                ve.tensor_tensor(wol[:, b, :, :], raw_o[:, b, :, :], woh[:, b, :, :].bitcast(F32),
                                 ALU.subtract).then_inc(wo_lo, 1)

            def relu_low(b, v):
                for k in range(UF):
                    dve.wait_ge(h_hi, UF * v + k + 1)
                    stt(out=hl[:, b, k, :], in0=bank(k, SLOTS), scalar=0.0, in1=hh[:, b, k, :].bitcast(F32),
                        op0=ALU.max, op1=ALU.subtract).then_inc(h_lo, 1)

            def gated_low(pr):
                def add(g):
                    dve.wait_ge(c_mm, NT * pr + g + 1)
                    ve.tensor_tensor(xs[:, g, :], bank(6 + g % 2, D), xs[:, g, :], ALU.add).then_inc(c_added, 1)

                for g in range(NT):
                    dve.wait_ge(c_hi, NT * pr + g + 1)
                    if g >= 2:
                        dve.wait_ge(c_mm, NT * pr + g - 1)
                    stt(out=cl[:, g % 2, :], in0=comb[:, g, :], scalar=gsc[:, g:g + 1], in1=ch[:, g % 2, :].bitcast(F32),
                        op0=ALU.mult, op1=ALU.subtract).then_inc(c_lo, 1)
                    if g > 0:
                        add(g - 1)
                add(NT - 1)

            def pair(pr, first=False, last=False):
                for k in range(PU):
                    v = PU * pr + k
                    relu_low(k % 2, v)
                    if k == 2 and not first:
                        gated_low(pr - 1)
                    if not (last and k + 2 >= PU):
                        split_wi(k % 2, v + 2)
                    if not (last and k + 1 >= PU):
                        split_wo((k + 1) % 2, v + 1)

            split_wi(0, 0)
            split_wi(1, 1)
            split_wo(0, 0)
            pair(0, first=True)
            with dve.Fori(1, PAIRS - 1) as q:
                pair(q)
            pair(PAIRS - 1, last=True)
            gated_low(PAIRS - 1)


_INS = ['x', 'L0_conv_w_qkv', 'L0_conv_b_qkv', 'L0_conv_w_proj', 'L0_conv_b_proj', 'L0_conv_rel_pos_h',
        'L0_conv_rel_pos_w', 'L0_ffn_w_router', 'L0_ffn_wi', 'L0_ffn_wo']


def kernel(**inputs):
    import numpy as _np
    import concourse.bacc as _bacc
    from concourse import mybir as _mybir
    from concourse.bass_utils import run_bass_kernel_spmd as _run

    arrays = {f"in_{n}": _np.ascontiguousarray(inputs[n]) for n in _INS}
    key = _np.arange(SIDE * SIDE)
    arrays["c_ident"] = _np.eye(P, dtype=_np.float32)
    arrays["c_flip"] = _np.eye(2 * SIDE - 1, dtype=_np.float32)[::-1].copy()
    arrays["c_onehot"] = _np.concatenate([
        (key[None, :] // SIDE == _np.arange(SIDE)[:, None]), (key[None, :] % SIDE == _np.arange(SIDE)[:, None]),
    ]).astype(_np.float32)
    arrays["c_before"] = _np.triu(_np.ones((P, P), _np.float32))
    experts = arrays["in_L0_ffn_wi"].shape[0]
    slots = max(int(2 * 1.25 * P / experts), 4)
    arrays["c_slots"] = _np.tile(_np.arange(1, slots + 1, dtype=_np.float32), (P, 1))

    nc = _bacc.Bacc("TRN2", target_bir_lowering=False, num_devices=1)
    args = [nc.dram_tensor(n, a.shape, _mybir.dt.from_np(a.dtype), kind="ExternalInput").ap() for n, a in arrays.items()]
    out = nc.dram_tensor("out_0", arrays["in_x"].shape, F32, kind="ExternalOutput").ap()
    metaformer_layer(nc, *args, out)
    r = _run(nc, [arrays], core_ids=[0])
    return r.results[0]["out_0"]
```

```python
from contextlib import ExitStack

import concourse.bass as bass
from concourse import mybir

ALU = mybir.AluOpType
ACT = mybir.ActivationFunctionType
AX_X = mybir.AxisListType.X
F32 = mybir.dt.float32
F32R = mybir.dt.float32r
U32 = mybir.dt.uint32

P = 128
BANK = 512
SIDE = 32
LN_C_EPS = 1e-6
LN_T_EPS = 1e-5


def metaformer_layer(nc, x, w_qkv, b_qkv, w_proj, b_proj, rel_pos_h, rel_pos_w, w_router, wi, wo,
                     ident_c, flip_c, onehot_c, tri_c, slot_c, out):
    T, D = SIDE * SIDE, x.shape[3]
    NT, DC = T // P, D // P
    HD = rel_pos_h.shape[1]
    NH = D // HD
    HPG = P // HD
    NREL = rel_pos_h.shape[0]
    E, _, F = wi.shape
    C = max(int(2 * 1.25 * P / E), 4)
    SLOTS = NT * C
    SCALE = float(HD) ** -0.5
    UF = 3
    UNITS = F // (UF * P)
    PAIRS = E // 2
    PU = 2 * UNITS
    PS = 2 * C
    assert T == 8 * P and HD == 32 and NH == 12 and E == 8 and NT == 8 and UNITS * UF * P == F

    x_v = x.rearrange("a h w d -> (a h w) d").rearrange("(t p) d -> p t d", p=P)
    out_v = out.rearrange("a h w d -> (a h w) d").rearrange("(t p) d -> p t d", p=P)
    wi_v = wi.rearrange("e (c p) (s f) -> e s p c f", p=P, s=UNITS)
    wo_v = wo.rearrange("e (s k p) d -> e s p k d", p=P, s=UNITS)

    at = [(nc.sbuf_base + 63) // 64 * 64]

    def room(nbytes):
        here = at[0]
        at[0] += (nbytes + 31) // 32 * 32
        return here

    def place(name, shape, dt, offset):
        return nc.alloc_sbuf_tensor_at(name, shape, dt, offset=offset)

    def new(name, shape, dt=F32):
        n = 4
        for s in shape[1:]:
            n *= s
        return place(name, shape, dt, room(n))

    TD = 4 * NT * D
    x0 = room(TD)
    xs = place("xs", [P, NT, D], F32, x0)
    w0 = room(4 * DC * D)
    wpj = place("wpj", [P, DC, D], F32, w0)
    dpc = place("dpc", [PS, NT, P], F32R, w0)
    ident = new("ident", [P, P])
    ones = new("ones", [P, P])
    tri = new("tri", [P, P])
    slot1 = new("slot1", [P, C])
    flip = new("flip", [NREL, NREL])
    bqk = new("bqk", [P, 2 * DC])
    wrt = new("wrt", [P, DC, E])
    stats = new("stats", [P, NT, 6])
    mv = new("mv", [P, NT, 2])
    veps = new("veps", [P, NT])
    std = new("std", [P, NT])
    rstd = new("rstd", [P, NT])
    gsl = new("gsl", [PS, PAIRS * NT])
    gsc = new("gsc", [PS, NT])
    base = at[0]

    u1, u2 = room(TD), room(TD)
    xn = place("xn", [P, NT, D], F32, u1)
    qf = place("qf", [P, DC, T], F32, u1)
    attn = place("attn", [P, NT, D], F32, u1)
    xnT = place("xnT", [P, DC, T], F32, u2)
    onehot = place("onehot", [P, T], F32, u2)
    attnT = place("attnT", [P, DC, T], F32, u2)
    u3 = room(4 * DC * 3 * D)
    wqkv = place("wqkv", [P, DC, 3 * D], F32, u3)
    prob = place("prob", [P, 2, T], F32, u3)
    b4 = room(4 * D)
    bv = place("bv", [P, D], F32, b4)
    mneg = place("mneg", [NT, P], F32R, b4)
    rl = place("rl", [P, 2, NT // 2], F32, b4 + 4 * P)
    bpj = new("bpj", [P, D])
    qh, ql = (new(n, [P, DC, T], F32R) for n in ("qh", "ql"))
    kp = new("kp", [P, 2, DC, T], F32R)
    rel = [new(n, [P, 2, DC, T], F32R) for n in ("relh", "relw")]
    v0 = room(TD)
    vt = place("vt", [P, NT, D], F32, v0)
    rst = place("rst", [P, 2, BANK], F32, v0)
    qst = [new("qst0", [P, 2, T], F32R), new("qst1", [P, 2, T], F32R), place("qst2", [P, 2, T], F32R, x0)]
    kst = [new("kst0", [P, 2, T], F32R), new("kst1", [P, 2, T], F32R), place("kst2", [P, 2, T], F32R, x0 + 8 * T)]
    o4 = room(4 * 2 * BANK)
    osb = place("osb", [P, BANK], F32, o4)
    vh = [new("vh0", [P, NT, 2 * HD]), new("vh1", [P, NT, 2 * HD]), place("vh2", [P, NT, 2 * HD], F32, o4 + 4 * BANK)]
    bd = place("bd", [P, 2, HPG, NREL], F32, o4)
    rhalf = new("rhalf", [P, NT, 2])
    rmax = new("rmax", [P, NT])
    rp = place("rp", [NREL, 2, HPG, HD], F32, o4 + 4 * BANK)
    b6 = place("b6", [2 * DC, P], F32, o4 + 6 * BANK)
    top = at[0]

    at[0] = base
    e1, e2, e3 = room(TD), room(TD), room(2 * TD)
    tn = place("tn", [P, NT, D], F32, e1)
    dg = place("dg", [P, NT, E, C], F32, e1)
    tnT = place("tnT", [P, DC, T], F32, e2)
    hh = place("hh", [P, 2, UF, SLOTS], F32R, e1)
    hl = place("hl", [P, 2, UF, SLOTS], F32R, e1 + 4 * 2 * UF * SLOTS)
    th = place("th", [P, NT, D], F32R, e3)
    tl = place("tl", [P, NT, D], F32R, e3 + TD)
    eoT = place("eoT", [P, DC, NT, 2, C], F32, e3)
    ch = place("ch", [PS, 2, D], F32R, e3 + 8 * DC * SLOTS)
    cl = place("cl", [PS, 2, D], F32R, e3 + 8 * DC * SLOTS + 8 * D)
    assert 8 * DC * SLOTS + 16 * D <= 2 * TD and 16 * UF * SLOTS <= 2 * TD
    dsp = new("dsp", [P, NT, E, C], F32R)
    dpt = new("dpt", [PS, PAIRS, NT, P], F32R)
    xeh, xel = (new(n, [P, DC, E, SLOTS], F32R) for n in ("xeh", "xel"))
    raw_i = new("raw_i", [P, 2, DC, UF * P])
    raw_o = new("raw_o", [P, 2, UF, D])
    wih, wil = (new(n, [P, 2, DC, UF * P], F32R) for n in ("wih", "wil"))
    woh, wol = (new(n, [P, 2, UF, D], F32R) for n in ("woh", "wol"))
    end, at[0] = at[0], at[0] - 8 * UF * D
    lg, ex, pr, mk1, mk2, gate, cm1, cm2, pos = (
        new(n, [P, NT, E]) for n in ("lg", "ex", "pr", "mk1", "mk2", "gate", "cm1", "cm2", "pos"))
    top8 = new("top8", [P, NT, 8])
    idx8 = new("idx8", [P, NT, 8], U32)
    idxf = new("idxf", [P, NT, 2])
    lmax, lsum, lrec = (new(n, [P, NT]) for n in ("lmax", "lsum", "lrec"))
    assert at[0] <= end and max(top, end) <= nc.sbuf_usable_end

    ctx = ExitStack()
    with ctx:
        ps = ctx.enter_context(nc.psum_tensor("ps", [P, 8 * BANK], F32))

        def bank(i, n=BANK):
            return ps[:, i * BANK:i * BANK + n]

        def sem(name):
            return ctx.enter_context(nc.semaphore(name))

        def wait(eng, s, value):
            if not isinstance(value, int) or value > 0:
                eng.wait_ge(s, value)

        x_in = [sem("x_in0"), sem("x_in1")]
        small_in, wqkv_in, wpj_in = sem("small_in"), sem("wqkv_in"), sem("wpj_in")
        raw_i_in = [sem("raw_i_in0"), sem("raw_i_in1")]
        raw_o_in = [sem("raw_o_in0"), sem("raw_o_in1")]
        ln_step, ln_var, ln_std = sem("ln_step"), sem("ln_var"), sem("ln_std")
        xn_ready, ones_set, bd_zero, rp_turned, bd_ready = (
            sem(n) for n in ("xn_ready", "ones_set", "bd_zero", "rp_turned", "bd_ready"))
        xb_ready, k_rows, rows_set = sem("xb_ready"), sem("k_rows"), sem("rows_set")
        turned, turn_act, turn_dve = sem("turned"), sem("turn_act"), sem("turn_dve")
        proj_mm, q_act, hi_act, lo_dve, v_mm, v_dve = (
            sem(n) for n in ("proj_mm", "q_act", "hi_act", "lo_dve", "v_mm", "v_dve"))
        rel_products_mm, rel_copied, rel_mm, rel_act, rel_dve = (
            sem(n) for n in ("rel_products_mm", "rel_copied", "rel_mm", "rel_act", "rel_dve"))
        heads_in = [sem(f"heads_in{b}") for b in range(3)]
        vh_ready, max_mm, max_red, max_whole, max_turned, mneg_ready, mrow_in = (
            sem(n) for n in ("vh_ready", "max_mm", "max_red", "max_whole", "max_turned", "mneg_ready", "mrow_in"))
        s_mm, exp_done, pv_mm, o_copied, o_turned, o_rec, o_normed = (
            sem(n) for n in ("s_mm", "exp_done", "pv_mm", "o_copied", "o_turned", "o_rec", "o_normed"))
        wproj_mm, x1_ready = sem("wproj_mm"), sem("x1_ready")
        th_ready, tl_ready, logits_mm, rt_step, ex_ready, masks_ready, count_mm = (
            sem(n) for n in ("th_ready", "tl_ready", "logits_mm", "rt_step", "ex_ready", "masks_ready", "count_mm"))
        dsp_ready, dg_ready, gsl_mm, gsl_ready = (
            sem(n) for n in ("dsp_ready", "dg_ready", "gsl_mm", "gsl_ready"))
        dpt_mm, dpt_act, dpt_dve, xe_mm, xe_act, xe_dve = (
            sem(n) for n in ("dpt_mm", "dpt_act", "dpt_dve", "xe_mm", "xe_act", "xe_dve"))
        wi_hi, wi_lo, wo_hi, wo_lo = (sem(n) for n in ("wi_hi", "wi_lo", "wo_hi", "wo_lo"))
        h_mm, h_hi, h_lo, y_mm, eo_ready = (sem(n) for n in ("h_mm", "h_hi", "h_lo", "y_mm", "eo_ready"))
        pair_set, c_turned, c_hi, c_lo, c_mm, c_added, out_done = (
            sem(n) for n in ("pair_set", "c_turned", "c_hi", "c_lo", "c_mm", "c_added", "out_done"))

        block = ctx.enter_context(nc.Block())

        SMALL = [
            (flip[:, :], flip_c), (rp[:, 0, :, :], rel_pos_h.unsqueeze(1).broadcast_to([NREL, HPG, HD])),
            (rp[:, 1, :, :], rel_pos_w.unsqueeze(1).broadcast_to([NREL, HPG, HD])),
            (ident[:, :], ident_c), (b6[:, :], b_qkv[0:2 * D].rearrange("(m p) -> m p", p=P)),
            (bv[:, :], b_qkv[2 * D:3 * D].partition_broadcast(P)), (bpj[:, :], b_proj.partition_broadcast(P)),
            (tri[:, :], tri_c), (slot1[:, :], slot_c), (wrt[:, :, :], w_router.rearrange("(c p) e -> p c e", p=P)),
            (onehot[2 * SIDE:4 * SIDE, :], onehot_c),
        ]
        SMALL_IN = 16 * len(SMALL)
        HALF = NT // 2
        HEAD_IN = 16 * 6
        QK = [(kk, c, half) for c in range(DC) for kk in range(2) for half in range(2)]
        QK_BANKS = [6, 7, 4, 5]
        REL = [(kind, c, half) for c in range(DC) for kind in range(2) for half in range(2)]
        V_BANKS = [6, 7, 0, 1]

        def rel_views(part, n):
            kind, c, half = REL[n]
            b, w = bank(2 + n % 2), SIDE // 2
            if kind == 0:
                return rel[0][:, part, c, half * BANK:(half + 1) * BANK], b
            return (rel[1][:, part, c, :].rearrange("p (r w) -> p w r", w=SIDE)[:, half * w:(half + 1) * w, :],
                    b.rearrange("p (w r) -> p w r", w=w))

        @block.sync
        def _(sp):
            for n in range(2):
                sp.dma_start(xs[:, n * HALF:(n + 1) * HALF, :], x_v[:, n * HALF:(n + 1) * HALF, :]).then_inc(x_in[n], 16)
            for dst, src in SMALL:
                sp.dma_start(dst, src).then_inc(small_in, 16)
            sp.dma_start(wqkv[:, :, :], w_qkv.rearrange("(c p) n -> p c n", p=P)).then_inc(wqkv_in, 16)

            def gather_head(h):
                chunk, rows, b = h // HPG, slice(HD * (h % HPG), HD * (h % HPG + 1)), h % 3
                for made in (hi_act, lo_dve, rel_act, rel_dve):
                    sp.wait_ge(made, 4 * (chunk + 1))
                if h == 2:
                    sp.wait_ge(k_rows, 3)
                if h > 2:
                    sp.wait_ge(s_mm, 8 * (h - 2))
                both = [HD, 2, T]
                parts = [(qst[b][0:HD, :, :], qh[rows, chunk, :].unsqueeze(1).broadcast_to(both)),
                         (qst[b][HD:2 * HD, 0, :], ql[rows, chunk, :]),
                         (qst[b][2 * HD:3 * HD, :, :], rel[0][rows, :, chunk, :]),
                         (qst[b][3 * HD:4 * HD, :, :], rel[1][rows, :, chunk, :]),
                         (kst[b][0:HD, :, :], kp[rows, :, chunk, :]),
                         (kst[b][HD:2 * HD, 0, :], kp[rows, 0, chunk, :])]
                for dst, src in parts:
                    sp.dma_start(dst.bitcast(F32), src.bitcast(F32)).then_inc(heads_in[b], 16)

            def max_row(h):
                sp.wait_ge(mneg_ready, h + 1)
                sp.dma_start(qst[h % 3][HD:HD + 1, 1, :].rearrange("o (t q) -> o t q", q=P).bitcast(F32),
                             mneg[:, :].bitcast(F32)).then_inc(mrow_in, 16)

            for h in range(3):
                gather_head(h)
            for h in range(NH):
                max_row(h)
                if 3 <= h + 2 < NH:
                    gather_head(h + 2)

            sp.wait_ge(s_mm, 8 * NH)
            sp.dma_start(wpj[:, :, :], w_proj.rearrange("(c p) n -> p c n", p=P)).then_inc(wpj_in, 16)
            for n in range(2):
                sp.dma_start(xs[:, n * HALF:(n + 1) * HALF, :], x_v[:, n * HALF:(n + 1) * HALF, :]).then_inc(x_in[n], 16)

            def load_unit(e, s, u):
                b = s % 2
                wait(sp, wi_lo, u - 1)
                sp.wait_ge(x1_ready, NT)
                sp.dma_start(raw_i[:, b, :, :], wi_v[e, s]).then_inc(raw_i_in[b], 16)
                wait(sp, wo_lo, u - 1)
                sp.wait_ge(x1_ready, NT)
                sp.dma_start(raw_o[:, b, :, :], wo_v[e, s]).then_inc(raw_o_in[b], 16)

            for u in range(PU):
                load_unit(u // UNITS, u % UNITS, u)
            with sp.Fori(0, PAIRS - 1) as pr:
                for k in range(2):
                    for s in range(UNITS):
                        load_unit(2 * pr + 2 + k, s, PU * pr + PU + UNITS * k + s)

            for t in range(NT):
                sp.wait_ge(c_added, NT * (PAIRS - 1) + t + 1)
                sp.dma_start(out_v[:, t, :], xs[:, t, :]).then_inc(out_done, 16)
            sp.wait_ge(out_done, 16 * NT)

        @block.gpsimd
        def _(pool):
            nc.gpsimd.memset(ones[:, :], 1.0).then_inc(ones_set, 1)
            for b in range(2):
                nc.gpsimd.memset(vh[b][:, :, HD:2 * HD], 1.0).then_inc(ones_set, 1)
            pool.wait_ge(ones_set, 3)
            for b in range(2):
                nc.gpsimd.memset(qst[b][HD:2 * HD, 1, :].bitcast(F32), 0.0).then_inc(rows_set, 1)
                nc.gpsimd.memset(kst[b][HD:2 * HD, 1, :].bitcast(F32), 1.0).then_inc(rows_set, 1)
            pool.wait_ge(xn_ready, NT)
            nc.gpsimd.memset(qst[2][HD:2 * HD, 1, :].bitcast(F32), 0.0).then_inc(rows_set, 1)
            nc.gpsimd.memset(kst[2][HD:2 * HD, 1, :].bitcast(F32), 1.0).then_inc(rows_set, 1)
            pool.wait_ge(rows_set, 6)
            pool.wait_ge(rp_turned, 3)
            nc.gpsimd.memset(vh[2][:, :, HD:2 * HD], 1.0).then_inc(ones_set, 1)
            pool.wait_ge(ones_set, 4)
            pool.wait_ge(k_rows, 2)
            nc.gpsimd.tensor_copy(kst[2][2 * HD:4 * HD, :, :], kst[0][2 * HD:4 * HD, :, :].bitcast(F32)).then_inc(k_rows, 1)
            pool.wait_ge(k_rows, 3)
            pool.wait_ge(v_dve, NT)

            def head_values(h, b):
                wait(pool, pv_mm, 8 * (h - 2))
                nc.gpsimd.tensor_copy(vh[b][:, :, 0:HD], vt[:, :, bass.ts(h, HD)]).then_inc(vh_ready, 1)

            for b in range(3):
                head_values(b, b)
            with pool.Fori(1, NH // 3) as i:
                for b in range(3):
                    head_values(3 * i + b, b)

            for t in range(NT):
                pool.wait_ge(x_in[t // HALF], 32)
                nc.gpsimd.tensor_tensor(xs[:, t, :], xs[:, t, :], bpj[:, :], ALU.add).then_inc(xb_ready, 1)

            def set_pair(pr):
                wait(pool, c_mm, NT * pr)
                wait(pool, c_lo, NT * pr)
                nc.gpsimd.tensor_copy(dpc[:, :, :], dpt[:, pr, :, :].bitcast(F32)).then_inc(pair_set, 1)
                nc.gpsimd.tensor_copy(gsc[:, :], gsl[:, bass.ts(pr, NT)]).then_inc(pair_set, 1)

            pool.wait_ge(dpt_act, PAIRS)
            pool.wait_ge(dpt_dve, PAIRS)
            pool.wait_ge(gsl_ready, 1)
            set_pair(0)
            with pool.Fori(1, PAIRS) as pr:
                set_pair(pr)

        @block.tensor
        def _(pe):
            mm = nc.tensor.matmul

            pe.wait_ge(small_in, SMALL_IN)
            for kind in range(2):
                nc.tensor.transpose(bank(6)[:, NREL * kind:NREL * (kind + 1)],
                                    rp[:, kind, :, :].rearrange("p a b -> p (a b)"), flip[:, :]).then_inc(rp_turned, 1)
            nc.tensor.transpose(bank(6)[:, 2 * NREL:2 * NREL + 2 * DC], b6[:, :],
                                ident[0:2 * DC, 0:2 * DC]).then_inc(rp_turned, 1)

            def turn(src, ready, done):
                for half in range(2):
                    if ready is not None:
                        pe.wait_ge(*ready(half))
                    for c in range(DC):
                        for t in range(HALF):
                            last = nc.tensor.transpose(bank(half * DC + c)[:, t * P:(t + 1) * P],
                                                       src[:, half * HALF + t, c * P:(c + 1) * P], ident[:, :])
                        last.then_inc(turned, 1)

            turn(xn, lambda half: (xn_ready, HALF * (half + 1)), turned)

            pe.wait_ge(turn_act, DC)
            pe.wait_ge(turn_dve, DC)
            pe.wait_ge(bd_ready, 2)
            pe.wait_ge(wqkv_in, 16)

            def qk(n):
                kk, chunk, half = QK[n]
                if n >= 4:
                    was = QK[n - 4]
                    if was[0]:
                        pe.wait_ge(lo_dve, n - 3)
                    else:
                        pe.wait_ge(q_act, 2 * was[1] + was[2] + 1)
                m = kk * DC + chunk
                for c in range(DC):
                    last = mm(bank(QK_BANKS[n % 4]), wqkv[:, c, m * P:(m + 1) * P],
                              xnT[:, c, half * BANK:(half + 1) * BANK], start=c == 0, stop=c == DC - 1)
                last.then_inc(proj_mm, 1)

            def rel_products(n):
                kind, c, half = REL[n]
                wait(pe, rel_copied, n - 1)
                for t in range(HALF):
                    for j in range(HPG):
                        r = (half * HALF + t) * HPG + j
                        q_of_r = qf[:, c, r * SIDE:(r + 1) * SIDE] if kind == 0 else qf[:, c, r:T:SIDE]
                        last = mm(bank(n % 2)[j * SIDE:(j + 1) * SIDE, t * P:(t + 1) * P], q_of_r,
                                  bd[:, kind, :, SIDE - 1 - r:2 * SIDE - 1 - r], start=True, stop=True)
                last.then_inc(rel_products_mm, 1)

            def rel_turn(n):
                pe.wait_ge(rel_copied, n + 1)
                wait(pe, rel_dve, n - 1)
                for t in range(HALF):
                    last = nc.tensor.transpose(bank(2 + n % 2)[:, t * P:(t + 1) * P],
                                               rst[:, n % 2, t * P:(t + 1) * P], ident[:, :])
                last.then_inc(rel_mm, 1)

            def rel_terms(first, end):
                pe.wait_ge(q_act, end // 2)
                for n in range(first, end):
                    rel_products(n)
                    if n > first:
                        rel_turn(n - 1)
                rel_turn(end - 1)

            for n in range(4):
                qk(n)
            rel_terms(0, 4)
            for n in range(4, 4 * DC):
                qk(n)
            rel_terms(4, 4 * DC)
            pe.wait_ge(lo_dve, 4 * DC)

            def value_tile(t):
                wait(pe, v_dve, t - 3)
                for c in range(DC):
                    last = mm(bank(V_BANKS[t % 4], D), xnT[:, c, t * P:(t + 1) * P], wqkv[:, c, 2 * D:3 * D],
                              start=c == 0, stop=c == DC - 1)
                last.then_inc(v_mm, 1)

            NP = 2 * NT

            def max_scores(h, n, b, p):
                if p == 0:
                    pe.wait_ge(heads_in[b], HEAD_IN * (n + 1))
                wait(pe, max_red, NP * h + p - 1)
                t, half = p // 2, p % 2
                mm(bank(4 + half), qst[b][:, 0, t * P:(t + 1) * P], kst[b][:, 0, half * BANK:(half + 1) * BANK],
                   start=True, stop=True).then_inc(max_mm, 1)

            def turn_max(h):
                pe.wait_ge(max_whole, h + 1)
                wait(pe, o_normed, h - 1)
                nc.tensor.transpose(bank(7)[0:NT, 0:P], rmax[:, :], ident[:, :]).then_inc(max_turned, 1)

            def scores(h, b, t):
                if t == 0:
                    pe.wait_ge(mrow_in, 16 * (h + 1))
                wait(pe, exp_done, 8 * h + t - 1)
                for half in range(2):
                    for part in range(2):
                        last = mm(bank(2 * (t % 2) + half), kst[b][:, part, t * P:(t + 1) * P],
                                  qst[b][:, part, half * BANK:(half + 1) * BANK], start=part == 0, stop=part == 1)
                last.then_inc(s_mm, 1)

            def values(h, b, t):
                pe.wait_ge(exp_done, 8 * h + t + 1)
                if t == 0:
                    pe.wait_ge(vh_ready, h + 1)
                    wait(pe, o_copied, h)
                for half in range(2):
                    last = mm(bank(6)[2 * HD * half:2 * HD * (half + 1), :], vh[b][:, t, :],
                              prob[:, t % 2, half * BANK:(half + 1) * BANK], start=t == 0, stop=t == NT - 1)
                last.then_inc(pv_mm, 1)

            def turn_output(h):
                pe.wait_ge(o_copied, h + 1)
                for j in range(HALF):
                    last = nc.tensor.transpose(bank(7)[:, j * P:(j + 1) * P], osb[:, j * P:(j + 1) * P], ident[:, :])
                last.then_inc(o_turned, 1)

            PIECES = [(0, 3), (3, 6), (6, 9), (9, 12), (12, 15), (15, 16), (16, 16), (16, 16)]

            def head(h, n, b, first=False, last=False):
                nxt = (n + b // 2, (b + 1) % 3)
                for t in range(NT):
                    pieces = [] if last else list(range(*PIECES[t]))
                    if t == 6 and not last:
                        turn_max(h + 1)
                    if t == 2 and not first:
                        wait(pe, mneg_ready, h + 1)
                        turn_output(h - 1)
                    for p in pieces[:1]:
                        max_scores(h + 1, *nxt, p)
                    scores(h, b, t)
                    for p in pieces[1:2]:
                        max_scores(h + 1, *nxt, p)
                    if t > 0:
                        values(h, b, t - 1)
                    elif not first:
                        values(h - 1, (b - 1) % 3, NT - 1)
                    for p in pieces[2:]:
                        max_scores(h + 1, *nxt, p)

            pe.wait_ge(k_rows, 3)
            pe.wait_ge(rows_set, 6)
            for t in range(NT):
                value_tile(t)
                max_scores(0, 0, 0, 2 * t)
                max_scores(0, 0, 0, 2 * t + 1)
            turn_max(0)
            pe.wait_ge(rel_dve, 4 * DC)
            pe.wait_ge(v_dve, NT)
            head(0, 0, 0, first=True)
            with pe.Fori(0, (NH - 3) // 3) as i:
                for j in range(1, 4):
                    head(3 * i + j, i + j // 3, j % 3)
            head(NH - 2, (NH - 2) // 3, (NH - 2) % 3)
            head(NH - 1, (NH - 1) // 3, (NH - 1) % 3, last=True)
            values(NH - 1, (NH - 1) % 3, NT - 1)
            pe.wait_ge(o_normed, NH - 1)
            turn_output(NH - 1)

            pe.wait_ge(exp_done, 8 * NH)
            pe.wait_ge(o_normed, NH)
            turn(attn, None, turned)
            pe.wait_ge(turn_act, 2 * DC)
            pe.wait_ge(turn_dve, 2 * DC)
            pe.wait_ge(wpj_in, 16)
            for t in range(NT):
                for c in range(DC):
                    last = mm(bank((6 + t) % 8, D), attnT[:, c, t * P:(t + 1) * P], wpj[:, c, :],
                              start=c == 0, stop=c == DC - 1)
                last.then_inc(wproj_mm, 1)

            turn(tn, lambda half: (xn_ready, NT + HALF * (half + 1)), turned)
            pe.wait_ge(turn_act, 3 * DC)
            pe.wait_ge(turn_dve, 3 * DC)
            for g in range(NT):
                for c in range(DC):
                    last = mm(bank(6)[:, g * E:(g + 1) * E], tnT[:, c, g * P:(g + 1) * P], wrt[:, c, :],
                              start=c == 0, stop=c == DC - 1)
            last.then_inc(logits_mm, 1)
            pe.wait_ge(masks_ready, 2)
            first_choice = mk1[:, :, :].rearrange("p g e -> p (g e)")
            second_choice = mk2[:, :, :].rearrange("p g e -> p (g e)")
            W = NT * E
            mm(bank(7, W), tri[:, :], first_choice, start=True, stop=True).then_inc(count_mm, 1)
            mm(bank(5, W), tri[:, :], second_choice, start=True, stop=False)
            mm(bank(5, W), ones[:, :], first_choice, start=False, stop=True).then_inc(count_mm, 1)

            pe.wait_ge(dsp_ready, 1)
            pe.wait_ge(th_ready, NT)
            pe.wait_ge(tl_ready, NT)
            n = 0
            for g in range(NT):
                slots = dsp[:, g, :, :].rearrange("p e c -> p (e c)")
                for c in range(DC):
                    for part in (th, tl):
                        if n >= 8:
                            pe.wait_ge((xe_act, xe_dve)[n % 2], n // 2 - 3)
                        mm(bank(n % 8, E * C), part[:, g, c * P:(c + 1) * P], slots,
                           start=True, stop=True).then_inc(xe_mm, 1)
                        n += 1
            n = 0
            pe.wait_ge(xe_act, NT * DC)
            pe.wait_ge(xe_dve, NT * DC)
            for pr in range(PAIRS):
                for half in range(2):
                    for q in range(HALF):
                        g = half * HALF + q
                        last = nc.tensor.transpose(
                            bank(n)[0:PS, q * P:(q + 1) * P],
                            dsp[:, g, 2 * pr:2 * pr + 2, :].rearrange("p e c -> p (e c)").bitcast(F32), ident[:, :])
                    last.then_inc(dpt_mm, 1)
                    n += 1
            pe.wait_ge(dg_ready, 1)
            pe.wait_ge(dpt_act, 1)
            for pr in range(PAIRS):
                for g in range(NT):
                    k = pr * NT + g
                    last = mm(bank(0)[0:PS, k:k + 1], dg[:, g, 2 * pr:2 * pr + 2, :].rearrange("p e c -> p (e c)"),
                              ones[:, 0:1], start=True, stop=True)
            last.then_inc(gsl_mm, 1)
            pe.wait_ge(gsl_ready, 1)
            pe.wait_ge(dpt_act, PAIRS)
            pe.wait_ge(dpt_dve, PAIRS)

            def hidden(e, b, v, between):
                pe.wait_ge(wi_hi, v + 1)
                pe.wait_ge(wi_lo, v + 1)
                for k in range(UF):
                    wait(pe, h_lo, UF * (v - 1) + k + 1)
                    terms = [(wih, xeh), (wih, xel), (wil, xeh)]
                    for c in range(DC):
                        for n, (w, xe) in enumerate(terms):
                            last = mm(bank(k, SLOTS), w[:, b, c, k * P:(k + 1) * P], xe[:, c, e, :],
                                      start=c == 0 and n == 0, stop=c == DC - 1 and n == 2)
                    last.then_inc(h_mm, 1)
                    between(k)

            def output(s, e, v, between):
                b = s % 2
                pe.wait_ge(wo_hi, v + 1)
                pe.wait_ge(wo_lo, v + 1)
                if s == 0:
                    wait(pe, eo_ready, DC * e)
                for k in range(UF):
                    pe.wait_ge(h_lo, UF * v + k + 1)
                    for c in range(DC):
                        for n, (w, h) in enumerate([(woh, hh), (woh, hl), (wol, hh)]):
                            last = mm(bank(3 + c, SLOTS), w[:, b, k, c * P:(c + 1) * P], h[:, b, k, :],
                                      start=s == 0 and k == 0 and n == 0,
                                      stop=s == UNITS - 1 and k == UF - 1 and n == 2)
                    if k == UF - 1:
                        last.then_inc(y_mm, 1)
                    between(k)

            def combine(pr, g, turn_bank, sum_bank):
                if g < NT:
                    for c in range(DC):
                        last = nc.tensor.transpose(bank(turn_bank)[0:PS, c * P:(c + 1) * P],
                                                   eoT[:, c, g, :, :].rearrange("p e s -> p (e s)"), ident[:, :])
                    last.then_inc(c_turned, 1)
                if g > 0:
                    pe.wait_ge(c_lo, NT * pr + g)
                    mm(bank(sum_bank, D), dpc[:, g - 1, :], ch[:, (g - 1) % 2, :], start=True, stop=False)
                    mm(bank(sum_bank, D), dpc[:, g - 1, :], cl[:, (g - 1) % 2, :], start=False, stop=True).then_inc(c_mm, 1)

            def combine_one(pr, g):
                if g == 0:
                    pe.wait_ge(eo_ready, DC * (2 * pr + 2))
                    pe.wait_ge(pair_set, 2 * pr + 2)
                else:
                    pe.wait_ge(c_lo, NT * pr + g)
                    wait(pe, c_added, NT * pr + g - 1)
                combine(pr, g, 6, 7)

            def nothing(k):
                pass

            def pair(pr, first=False, last=False):
                for k in range(PU):
                    v = PU * pr + k
                    while_hidden, while_output = nothing, nothing
                    if not first and k == 1:
                        def while_hidden(j): combine_one(pr - 1, j)
                        def while_output(j): combine_one(pr - 1, UF + j)
                    if not first and k == 2:
                        def while_hidden(j): combine_one(pr - 1, 2 * UF + j)
                    if not (last and k == PU - 1):
                        hidden(2 * pr + (k + 1) // UNITS, (k + 1) % 2, v + 1, while_hidden)
                    output(k % UNITS, 2 * pr + k // UNITS, v, while_output)

            hidden(0, 0, 0, nothing)
            pair(0, first=True)
            with pe.Fori(1, PAIRS - 1) as pr:
                pair(pr)
            pair(PAIRS - 1, last=True)
            pe.wait_ge(eo_ready, DC * E)
            pe.wait_ge(pair_set, 2 * PAIRS)
            for g in range(NT + 1):
                if g >= 2:
                    pe.wait_ge(c_lo, NT * (PAIRS - 1) + g - 1)
                if g >= 3:
                    pe.wait_ge(c_added, NT * (PAIRS - 1) + g - 2)
                combine(PAIRS - 1, g, (6, 0)[g % 2], (7, 1)[(g - 1) % 2])

        @block.scalar
        def _(act):
            run = nc.scalar.activation

            def turn_back(dst, n):
                for k in range(0, 2 * DC, 2):
                    act.wait_ge(turned, 2 * DC * n + k + 1)
                    run(dst[:, k % DC, (k // DC) * BANK:(k // DC + 1) * BANK], bank(k), ACT.Copy).then_inc(turn_act, 1)

            act.wait_ge(small_in, SMALL_IN)
            for b in range(2):
                run(kst[b][2 * SIDE:4 * SIDE, :, :],
                    onehot[2 * SIDE:4 * SIDE, :].unsqueeze(1).broadcast_to([2 * SIDE, 2, T]), ACT.Copy).then_inc(k_rows, 1)
            act.wait_ge(ln_var, 1)
            run(std[:, :], veps[:, :], ACT.Sqrt).then_inc(ln_std, 1)
            act.wait_ge(k_rows, 2)
            turn_back(xnT, 0)
            act.wait_ge(bd_ready, 2)
            def units(first, end):
                for n in range(first, end):
                    kk, c, half = QK[n]
                    cols = slice(half * BANK, (half + 1) * BANK)
                    act.wait_ge(proj_mm, n + 1)
                    if kk:
                        run(kp[:, 0, c, cols], bank(QK_BANKS[n % 4]), ACT.Identity, bias=bqk[:, DC + c:DC + c + 1]).then_inc(hi_act, 1)
                    else:
                        run(qf[:, c, cols], bank(QK_BANKS[n % 4]), ACT.Identity, bias=bqk[:, c:c + 1]).then_inc(q_act, 1)
                        act.wait_ge(q_act, 2 * c + half + 1)
                        run(qh[:, c, cols], qf[:, c, cols], ACT.Copy, scale=SCALE).then_inc(hi_act, 1)

            def rel_high(n):
                act.wait_ge(rel_mm, n + 1)
                dst, src = rel_views(0, n)
                run(dst, src, ACT.Copy).then_inc(rel_act, 1)

            def rels(first, end):
                for n in range(first, end):
                    act.wait_ge(rel_products_mm, n + 1)
                    wait(act, rel_mm, n - 1)
                    run(rst[:, n % 2, :], bank(n % 2), ACT.Copy).then_inc(rel_copied, 1)
                    if n > first:
                        rel_high(n - 1)
                rel_high(end - 1)

            units(0, 4)
            rels(0, 4)
            units(4, 4 * DC)
            rels(4, 4 * DC)

            def exps(h, first=False):
                for t in range(NT):
                    act.wait_ge(s_mm, 8 * h + t + 1)
                    wait(act, pv_mm, 8 * h + t - 1)
                    run(prob[:, t % 2, :], ps[:, 2 * (t % 2) * BANK:2 * (t % 2 + 1) * BANK], ACT.Exp).then_inc(exp_done, 1)
                    if t == 0 and not first:
                        copy_output(h - 1)

            def copy_output(h):
                act.wait_ge(pv_mm, 8 * h + 8)
                run(osb[:, :], bank(6), ACT.Copy).then_inc(o_copied, 1)

            exps(0, first=True)
            with act.Fori(1, NH) as h:
                exps(h)
            copy_output(NH - 1)
            turn_back(attnT, 1)

            act.wait_ge(ln_var, 2)
            run(std[:, :], veps[:, :], ACT.Sqrt).then_inc(ln_std, 1)
            for t in range(NT):
                act.wait_ge(xn_ready, NT + t + 1)
                run(th[:, t, :], tn[:, t, :], ACT.Copy).then_inc(th_ready, 1)
            turn_back(tnT, 2)
            act.wait_ge(rt_step, 2)
            run(ex[:, :, :], lg[:, :, :], ACT.Exp).then_inc(ex_ready, 1)
            n = 0
            for g in range(NT):
                for c in range(DC):
                    act.wait_ge(xe_mm, n + 1)
                    run(xeh[:, c, :, g * C:(g + 1) * C],
                        bank(n % 8, E * C).rearrange("p (e c) -> p e c", e=E), ACT.Copy).then_inc(xe_act, 1)
                    n += 2
            for pr in range(PAIRS):
                act.wait_ge(dpt_mm, 2 * pr + 1)
                run(dpt[:, pr, 0:HALF, :].rearrange("p g s -> p (g s)"), bank(2 * pr)[0:PS, :], ACT.Copy).then_inc(dpt_act, 1)

            def split_wi(b, v, n):
                act.wait_ge(raw_i_in[b], 16 * (n + 1))
                wait(act, h_mm, UF * (v - 1))
                run(wih[:, b, :, :], raw_i[:, b, :, :], ACT.Copy).then_inc(wi_hi, 1)

            def split_wo(b, v, n):
                act.wait_ge(raw_o_in[b], 16 * (n + 1))
                wait(act, y_mm, v - 1)
                run(woh[:, b, :, :], raw_o[:, b, :, :], ACT.Copy).then_inc(wo_hi, 1)

            def relu(b, v, k):
                act.wait_ge(h_mm, UF * v + k + 1)
                run(hh[:, b, k, :], bank(k, SLOTS), ACT.Relu).then_inc(h_hi, 1)

            def leave(pr, k):
                act.wait_ge(y_mm, UNITS * (2 * pr + k + 1))
                wait(act, c_turned, NT * pr)
                for c in range(DC):
                    run(eoT[:, c, :, k, :], bank(3 + c, SLOTS).rearrange("p (g s) -> p g s", s=C), ACT.Copy).then_inc(eo_ready, 1)

            def gated(pr, g, turn_bank=6):
                act.wait_ge(c_turned, NT * pr + g + 1)
                if g == 0:
                    act.wait_ge(pair_set, 2 * pr + 2)
                if g >= 2:
                    act.wait_ge(c_mm, NT * pr + g - 1)
                run(ch[:, g % 2, :], bank(turn_bank, D)[0:PS, :], ACT.Copy, scale=gsc[:, g:g + 1]).then_inc(c_hi, 1)

            def pair(pr, first=False, last=False):
                for k in range(PU):
                    v = PU * pr + k
                    wait(act, y_mm, v - 1)
                    for j in range(UF):
                        relu(k % 2, v, j)
                        if not first and k == 2:
                            gated(pr - 1, j)
                        if not first and k == 3 and j < 2:
                            gated(pr - 1, 2 * UF + j)
                    if k == 0 and not first:
                        leave(pr - 1, 1)
                    if k == UNITS:
                        leave(pr, 0)
                    if not (last and k + 2 >= PU):
                        split_wi(k % 2, v + 2, PU // 2 * pr + k // 2 + 1)
                    if not first and k == 2:
                        gated(pr - 1, 3)
                        gated(pr - 1, 4)
                    if not (last and k + 1 >= PU):
                        split_wo((k + 1) % 2, v + 1, PU // 2 * pr + (k + 1) // 2)
                    if not first and k == 2:
                        gated(pr - 1, 5)

            split_wi(0, 0, 0)
            split_wi(1, 1, 0)
            split_wo(0, 0, 0)
            pair(0, first=True)
            with act.Fori(1, PAIRS - 1) as pr:
                pair(pr)
            pair(PAIRS - 1, last=True)
            leave(PAIRS - 1, 1)
            for g in range(NT):
                gated(PAIRS - 1, g, (6, 0)[g % 2])

        @block.vector
        def _(dve):
            ve = nc.vector
            stt = ve.scalar_tensor_tensor

            def norm(src, dst, eps, n, ready):
                s0 = n * 3 * NT
                for t in range(NT):
                    ready(t)
                    ve.bn_stats(stats[:, t, :], src[:, t, :]).then_inc(ln_step, 1)
                dve.wait_ge(ln_step, s0 + NT)
                for t in range(NT):
                    ve.bn_aggr(mv[:, t, :], stats[:, t, :]).then_inc(ln_step, 1)
                dve.wait_ge(ln_step, s0 + 2 * NT)
                ve.tensor_scalar(veps[:, :], mv[:, :, 1], eps, None, ALU.add).then_inc(ln_var, 1)
                dve.wait_ge(ln_std, n + 1)
                ve.reciprocal(rstd[:, :], std[:, :]).then_inc(ln_step, NT)
                dve.wait_ge(ln_step, s0 + 3 * NT)
                for t in range(NT):
                    ve.tensor_scalar(dst[:, t, :], src[:, t, :], mv[:, t, 0:1], rstd[:, t:t + 1],
                                     ALU.subtract, ALU.mult).then_inc(xn_ready, 1)

            def turn_back(dst, n):
                for k in range(1, 2 * DC, 2):
                    dve.wait_ge(turned, 2 * DC * n + k + 1)
                    ve.tensor_copy(dst[:, k % DC, (k // DC) * BANK:(k // DC + 1) * BANK], bank(k)).then_inc(turn_dve, 1)

            ve.memset(bd[:, :, :, :], 0.0).then_inc(bd_zero, 1)
            norm(xs, xn, LN_C_EPS, 0, lambda t: dve.wait_ge(x_in[t // HALF], 16))
            dve.wait_ge(bd_zero, 1)
            dve.wait_ge(rp_turned, 3)
            ve.tensor_copy(bqk[:, :], bank(6)[:, 2 * NREL:2 * NREL + 2 * DC]).then_inc(bd_ready, 1)
            for j in range(HPG):
                rows = slice(HD * j, HD * (j + 1))
                last = ve.tensor_copy(bd[rows, :, j, :], bank(6, 2 * NREL)[rows, :].rearrange("p (k r) -> p k r", k=2))
            last.then_inc(bd_ready, 1)
            dve.wait_ge(k_rows, 2)
            turn_back(xnT, 0)
            def units(first, end):
                for n in range(first, end):
                    kk, c, half = QK[n]
                    cols = slice(half * BANK, (half + 1) * BANK)
                    dve.wait_ge(hi_act, n + 1)
                    if kk:
                        stt(out=kp[:, 1, c, cols], in0=bank(QK_BANKS[n % 4]), scalar=bqk[:, DC + c:DC + c + 1],
                            in1=kp[:, 0, c, cols].bitcast(F32), op0=ALU.add, op1=ALU.subtract).then_inc(lo_dve, 1)
                    else:
                        stt(out=ql[:, c, cols], in0=qf[:, c, cols], scalar=SCALE, in1=qh[:, c, cols].bitcast(F32),
                            op0=ALU.mult, op1=ALU.subtract).then_inc(lo_dve, 1)

            def rels(first, end):
                for n in range(first, end):
                    dve.wait_ge(rel_act, n + 1)
                    dst, src = rel_views(1, n)
                    ve.tensor_tensor(dst, src, rel_views(0, n)[0].bitcast(F32), ALU.subtract).then_inc(rel_dve, 1)

            units(0, 4)
            rels(0, 4)
            units(4, 4 * DC)
            rels(4, 4 * DC)

            def reduce_max(h, p):
                dve.wait_ge(max_mm, 2 * NT * h + p + 1)
                ve.tensor_reduce(rhalf[:, p // 2, p % 2:p % 2 + 1], bank(4 + p % 2), AX_X, ALU.max).then_inc(max_red, 1)

            def negate_max(h):
                dve.wait_ge(max_red, 2 * NT * (h + 1))
                ve.tensor_reduce(rmax[:, :], rhalf[:, :, :], AX_X, ALU.max).then_inc(max_whole, 1)
                dve.wait_ge(max_turned, h + 1)
                wait(dve, mrow_in, 16 * h)
                ve.tensor_scalar(mneg[:, :], bank(7)[0:NT, 0:P], -1.0, None, ALU.mult).then_inc(mneg_ready, 1)

            def normalise(h):
                turned_o = bank(7).rearrange("p (j s c) -> p s j c", s=2, c=2 * HD)
                dve.wait_ge(o_turned, h + 1)
                ve.reciprocal(rl[:, :, :], turned_o[:, :, :, HD]).then_inc(o_rec, 1)
                dve.wait_ge(o_rec, h + 1)
                ve.tensor_tensor(attn[:, :, bass.ts(h, HD)].rearrange("p (s j) d -> p s j d", s=2),
                                 turned_o[:, :, :, 0:HD],
                                 rl[:, :, :].unsqueeze(3).broadcast_to([P, 2, HALF, HD]), ALU.mult).then_inc(o_normed, 1)

            def head(h, first=False):
                for p in range(2 * NT):
                    if p == 6 and not first:
                        normalise(h - 1)
                    reduce_max(h + 1, p)
                negate_max(h + 1)

            for t in range(NT):
                dve.wait_ge(v_mm, t + 1)
                ve.tensor_tensor(vt[:, t, :], bank(V_BANKS[t % 4], D), bv[:, :], ALU.add).then_inc(v_dve, 1)
                reduce_max(0, 2 * t)
                reduce_max(0, 2 * t + 1)
            negate_max(0)
            head(0, first=True)
            with dve.Fori(1, NH - 1) as h:
                head(h)
            normalise(NH - 2)
            normalise(NH - 1)
            turn_back(attnT, 1)

            dve.wait_ge(xb_ready, NT)
            for t in range(NT):
                dve.wait_ge(wproj_mm, t + 1)
                ve.tensor_tensor(xs[:, t, :], bank((6 + t) % 8, D), xs[:, t, :], ALU.add).then_inc(x1_ready, 1)
            norm(xs, tn, LN_T_EPS, 1, lambda t: dve.wait_ge(x1_ready, t + 1))
            for t in range(NT):
                dve.wait_ge(th_ready, t + 1)
                ve.tensor_tensor(tl[:, t, :], tn[:, t, :], th[:, t, :].bitcast(F32), ALU.subtract).then_inc(tl_ready, 1)
            turn_back(tnT, 2)

            steps = [0]

            def step(ins):
                steps[0] += 1
                ins.then_inc(rt_step, 1)
                dve.wait_ge(rt_step, steps[0])

            def over(v, n):
                return v.unsqueeze(len(v.shape)).broadcast_to([*v.shape, n])

            logits = bank(6, NT * E).rearrange("p (g e) -> p g e", e=E)
            dve.wait_ge(logits_mm, 1)
            step(ve.tensor_reduce(lmax[:, :], logits, AX_X, ALU.max))
            step(ve.tensor_tensor(lg[:, :, :], logits, over(lmax[:, :], E), ALU.subtract))
            dve.wait_ge(ex_ready, 1)
            step(ve.tensor_reduce(lsum[:, :], ex[:, :, :], AX_X, ALU.add))
            step(ve.reciprocal(lrec[:, :], lsum[:, :]))
            step(ve.tensor_tensor(pr[:, :, :], ex[:, :, :], over(lrec[:, :], E), ALU.mult))
            for g in range(NT):
                last = ve.max(top8[:, g, :], pr[:, g, :])
                if g < NT - 1:
                    last.then_inc(rt_step, 1)
                    steps[0] += 1
            step(last)
            for g in range(NT):
                last = ve.max_index(idx8[:, g, :], top8[:, g, :], pr[:, g, :])
                if g < NT - 1:
                    last.then_inc(rt_step, 1)
                    steps[0] += 1
            step(last)
            step(ve.tensor_copy(idxf[:, :, :], idx8[:, :, 0:2]))
            step(ve.tensor_scalar(idxf[:, :, :], idxf[:, :, :], 1.0, None, ALU.add))
            number = slot1[:, 0:E].unsqueeze(1).broadcast_to([P, NT, E])
            ve.tensor_tensor(mk1[:, :, :], number, idxf[:, :, 0:1].broadcast_to([P, NT, E]), ALU.is_equal).then_inc(masks_ready, 1)
            ve.tensor_tensor(mk2[:, :, :], number, idxf[:, :, 1:2].broadcast_to([P, NT, E]), ALU.is_equal).then_inc(masks_ready, 1)
            dve.wait_ge(masks_ready, 2)
            step(ve.tensor_tensor(gate[:, :, :], mk1[:, :, :], top8[:, :, 0:1].broadcast_to([P, NT, E]), ALU.mult))
            step(ve.tensor_tensor(cm1[:, :, :], mk2[:, :, :], top8[:, :, 1:2].broadcast_to([P, NT, E]), ALU.mult))
            step(ve.tensor_tensor(gate[:, :, :], gate[:, :, :], cm1[:, :, :], ALU.add))
            dve.wait_ge(count_mm, 2)
            step(ve.tensor_tensor(cm1[:, :, :], bank(7, NT * E).rearrange("p (g e) -> p g e", e=E), mk1[:, :, :], ALU.mult))
            step(ve.tensor_tensor(cm2[:, :, :], bank(5, NT * E).rearrange("p (g e) -> p g e", e=E), mk2[:, :, :], ALU.mult))
            step(ve.tensor_tensor(pos[:, :, :], cm1[:, :, :], cm2[:, :, :], ALU.add))
            ge = [P, NT * E, C]
            ve.tensor_tensor(dsp[:, :, :, :].rearrange("p g e c -> p (g e) c"), slot1[:, :].unsqueeze(1).broadcast_to(ge),
                             over(pos[:, :, :].rearrange("p g e -> p (g e)"), C), ALU.is_equal).then_inc(dsp_ready, 1)
            dve.wait_ge(dsp_ready, 1)
            dve.wait_ge(turned, 6 * DC)
            ve.tensor_tensor(dg[:, :, :, :].rearrange("p g e c -> p (g e) c"),
                             dsp[:, :, :, :].rearrange("p g e c -> p (g e) c").bitcast(F32),
                             over(gate[:, :, :].rearrange("p g e -> p (g e)"), C), ALU.mult).then_inc(dg_ready, 1)
            n = 1
            for g in range(NT):
                for c in range(DC):
                    dve.wait_ge(xe_mm, n + 1)
                    ve.tensor_copy(xel[:, c, :, g * C:(g + 1) * C],
                                   bank(n % 8, E * C).rearrange("p (e c) -> p e c", e=E)).then_inc(xe_dve, 1)
                    n += 2
            for q in range(PAIRS):
                dve.wait_ge(dpt_mm, 2 * q + 2)
                ve.tensor_copy(dpt[:, q, HALF:NT, :].rearrange("p g s -> p (g s)"), bank(2 * q + 1)[0:PS, :]).then_inc(dpt_dve, 1)
            dve.wait_ge(gsl_mm, 1)
            ve.tensor_copy(gsl[:, :], bank(0)[0:PS, 0:PAIRS * NT]).then_inc(gsl_ready, 1)

            def split_wi(b, v):
                dve.wait_ge(wi_hi, v + 1)
                ve.tensor_tensor(wil[:, b, :, :], raw_i[:, b, :, :], wih[:, b, :, :].bitcast(F32),
                                 ALU.subtract).then_inc(wi_lo, 1)

            def split_wo(b, v):
                dve.wait_ge(wo_hi, v + 1)
                ve.tensor_tensor(wol[:, b, :, :], raw_o[:, b, :, :], woh[:, b, :, :].bitcast(F32),
                                 ALU.subtract).then_inc(wo_lo, 1)

            def relu_low(b, v, k):
                dve.wait_ge(h_hi, UF * v + k + 1)
                stt(out=hl[:, b, k, :], in0=bank(k, SLOTS), scalar=0.0, in1=hh[:, b, k, :].bitcast(F32),
                    op0=ALU.max, op1=ALU.subtract).then_inc(h_lo, 1)

            def combine(pr, g, turn_bank=6, sum_bank=7):
                if g < NT:
                    dve.wait_ge(c_hi, NT * pr + g + 1)
                    if g >= 2:
                        dve.wait_ge(c_mm, NT * pr + g - 1)
                    stt(out=cl[:, g % 2, :], in0=bank(turn_bank, D)[0:PS, :], scalar=gsc[:, g:g + 1],
                        in1=ch[:, g % 2, :].bitcast(F32), op0=ALU.mult, op1=ALU.subtract).then_inc(c_lo, 1)
                if g > 0:
                    dve.wait_ge(c_mm, NT * pr + g)
                    ve.tensor_tensor(xs[:, g - 1, :], bank(sum_bank, D), xs[:, g - 1, :], ALU.add).then_inc(c_added, 1)

            def pair(pr, first=False, last=False):
                for k in range(PU):
                    v = PU * pr + k
                    for j in range(UF):
                        relu_low(k % 2, v, j)
                        if not first and k == 2:
                            combine(pr - 1, j)
                        if not first and k == 3:
                            combine(pr - 1, 2 * UF + j)
                    if not (last and k + 2 >= PU):
                        split_wi(k % 2, v + 2)
                    if not first and k == 2:
                        combine(pr - 1, 3)
                        combine(pr - 1, 4)
                    if not (last and k + 1 >= PU):
                        split_wo((k + 1) % 2, v + 1)
                    if not first and k == 2:
                        combine(pr - 1, 5)

            split_wi(0, 0)
            split_wi(1, 1)
            split_wo(0, 0)
            pair(0, first=True)
            with dve.Fori(1, PAIRS - 1) as q:
                pair(q)
            pair(PAIRS - 1, last=True)
            for g in range(NT + 1):
                combine(PAIRS - 1, g, (6, 0)[g % 2], (7, 1)[(g - 1) % 2])


_INS = ['x', 'L0_conv_w_qkv', 'L0_conv_b_qkv', 'L0_conv_w_proj', 'L0_conv_b_proj', 'L0_conv_rel_pos_h',
        'L0_conv_rel_pos_w', 'L0_ffn_w_router', 'L0_ffn_wi', 'L0_ffn_wo']


def kernel(**inputs):
    import numpy as _np
    import concourse.bacc as _bacc
    from concourse import mybir as _mybir
    from concourse.bass_utils import run_bass_kernel_spmd as _run

    arrays = {f"in_{n}": _np.ascontiguousarray(inputs[n]) for n in _INS}
    key = _np.arange(SIDE * SIDE)
    arrays["c_ident"] = _np.eye(P, dtype=_np.float32)
    arrays["c_flip"] = _np.eye(2 * SIDE - 1, dtype=_np.float32)[::-1].copy()
    arrays["c_onehot"] = _np.concatenate([
        (key[None, :] // SIDE == _np.arange(SIDE)[:, None]), (key[None, :] % SIDE == _np.arange(SIDE)[:, None]),
    ]).astype(_np.float32)
    arrays["c_before"] = _np.triu(_np.ones((P, P), _np.float32))
    experts = arrays["in_L0_ffn_wi"].shape[0]
    slots = max(int(2 * 1.25 * P / experts), 4)
    arrays["c_slots"] = _np.tile(_np.arange(1, slots + 1, dtype=_np.float32), (P, 1))

    nc = _bacc.Bacc("TRN2", target_bir_lowering=False, num_devices=1)
    args = [nc.dram_tensor(n, a.shape, _mybir.dt.from_np(a.dtype), kind="ExternalInput").ap() for n, a in arrays.items()]
    out = nc.dram_tensor("out_0", arrays["in_x"].shape, F32, kind="ExternalOutput").ap()
    metaformer_layer(nc, *args, out)
    r = _run(nc, [arrays], core_ids=[0])
    return r.results[0]["out_0"]
```

```python
from contextlib import ExitStack

import concourse.bass as bass
from concourse import mybir

ALU = mybir.AluOpType
ACT = mybir.ActivationFunctionType
AX_X = mybir.AxisListType.X
F32 = mybir.dt.float32
F32R = mybir.dt.float32r
U32 = mybir.dt.uint32

P = 128
BANK = 512
SIDE = 32
LN_C_EPS = 1e-6
LN_T_EPS = 1e-5


def metaformer_layer(nc, x, w_qkv, b_qkv, w_proj, b_proj, rel_pos_h, rel_pos_w, w_router, wi, wo,
                     ident_c, flip_c, onehot_c, tri_c, slot_c, out):
    T, D = SIDE * SIDE, x.shape[3]
    NT, DC = T // P, D // P
    HD = rel_pos_h.shape[1]
    NH = D // HD
    HPG = P // HD
    NREL = rel_pos_h.shape[0]
    E, _, F = wi.shape
    C = max(int(2 * 1.25 * P / E), 4)
    SLOTS = NT * C
    SCALE = float(HD) ** -0.5
    UF = 3
    UNITS = F // (UF * P)
    PAIRS = E // 2
    PU = 2 * UNITS
    PS = 2 * C
    assert T == 8 * P and HD == 32 and NH == 12 and E == 8 and NT == 8 and UNITS * UF * P == F

    x_v = x.rearrange("a h w d -> (a h w) d").rearrange("(t p) d -> p t d", p=P)
    out_v = out.rearrange("a h w d -> (a h w) d").rearrange("(t p) d -> p t d", p=P)
    wi_v = wi.rearrange("e (c p) (s f) -> e s p c f", p=P, s=UNITS)
    wo_v = wo.rearrange("e (s k p) d -> e s p k d", p=P, s=UNITS)

    at = [(nc.sbuf_base + 63) // 64 * 64]

    def room(nbytes):
        here = at[0]
        at[0] += (nbytes + 31) // 32 * 32
        return here

    def place(name, shape, dt, offset):
        return nc.alloc_sbuf_tensor_at(name, shape, dt, offset=offset)

    def new(name, shape, dt=F32):
        n = 4
        for s in shape[1:]:
            n *= s
        return place(name, shape, dt, room(n))

    TD = 4 * NT * D
    x0 = room(TD)
    xs = place("xs", [P, NT, D], F32, x0)
    w0 = room(4 * DC * D)
    wvh = place("wvh", [P, DC, D], F32R, w0)
    dpc = place("dpc", [PS, NT, P], F32R, w0)
    ident = new("ident", [P, P])
    ones = new("ones", [P, P])
    tri = new("tri", [P, P])
    slot1 = new("slot1", [P, C])
    g0 = room(4 * NT * E)
    flip = place("flip", [NREL, NREL], F32, g0)
    gate = place("gate", [P, NT, E], F32, g0)
    bqk = new("bqk", [P, 2 * DC])
    wrt = new("wrt", [P, DC, E])
    stats = new("stats", [P, NT, 6])
    mv = new("mv", [P, NT, 2])
    veps = new("veps", [P, NT])
    std = new("std", [P, NT])
    rstd = new("rstd", [P, NT])
    gsl = new("gsl", [PS, PAIRS * NT])
    gsc = new("gsc", [PS, NT])
    base = at[0]

    u1, u2 = room(TD), room(TD)
    xn = place("xn", [P, NT, D], F32, u1)
    qf = place("qf", [P, DC, T], F32, u1)
    attn = place("attn", [P, NT, D], F32, u1)
    xnh, xnl = place("xnh", [P, DC, T], F32R, u2), place("xnl", [P, DC, T], F32R, x0)
    ath = place("ath", [P, DC, T], F32R, u2)
    u3 = room(4 * DC * 3 * D)
    v3 = u3 + 4 * DC * 2 * D
    wqk, wv = place("wqk", [P, DC, 2 * D], F32, u3), place("wv", [P, DC, D], F32, v3)
    wqkl, wvl = place("wqkl", [P, DC, 2 * D], F32R, u3), place("wvl", [P, DC, D], F32R, v3)
    prob = place("prob", [P, 2, T], F32, u3)
    mneg = place("mneg", [NT, P], F32R, u3 + 8 * T)
    rl = place("rl", [P, 2, NT // 2], F32, u3 + 8 * T + 4 * P)
    assert 8 * T + 4 * P + 4 * NT <= 4 * DC * 2 * D
    atl = place("atl", [P, DC, T], F32R, u3)
    bv = new("bv", [P, D])
    bpj = new("bpj", [P, D])
    qh, ql = (new(n, [P, DC, T], F32R) for n in ("qh", "ql"))
    kp = new("kp", [P, 2, DC, T], F32R)
    rel = [new(n, [P, 2, DC, T], F32R) for n in ("relh", "relw")]
    v0 = room(TD)
    vt = place("vt", [P, NT, D], F32, v0)
    rst = place("rst", [P, 2, BANK], F32, v0)
    onehot = place("onehot", [P, T], F32, v0 + 8 * BANK)
    q0, q1 = room(16 * T), room(16 * T)
    qst = [place(f"qst{b}", [P, 2, T], F32R, at_b) for b, at_b in enumerate((q0, q1, x0))]
    kst = [place(f"kst{b}", [P, 2, T], F32R, at_b + 8 * T) for b, at_b in enumerate((q0, q1, x0))]
    wqkh = place("wqkh", [P, DC, 2 * D], F32R, q1)
    wpj, wpl = (place(n, [P, DC, D], dt, q0) for n, dt in (("wpj", F32), ("wpl", F32R)))
    wph = place("wph", [P, DC, D], F32R, q0 + 8 * T)
    o4 = room(4 * 2 * BANK)
    osb = place("osb", [P, BANK], F32, o4)
    vh = [new("vh0", [P, NT, 2 * HD]), new("vh1", [P, NT, 2 * HD]), place("vh2", [P, NT, 2 * HD], F32, o4 + 4 * BANK)]
    bd = place("bd", [P, 2, HPG, NREL], F32, o4)
    rhalf = new("rhalf", [P, NT, 2])
    rmax = new("rmax", [P, NT])
    rp = place("rp", [NREL, 2, HPG, HD], F32, o4 + 4 * BANK)
    b6 = place("b6", [2 * DC, P], F32, o4 + 6 * BANK)
    top = at[0]

    at[0] = base
    e1, e2, e3 = room(TD), room(TD), room(2 * TD)
    tn = place("tn", [P, NT, D], F32, e1)
    tnT = place("tnT", [P, DC, T], F32, e2)
    hh = place("hh", [P, 2, UF, SLOTS], F32R, e1)
    hl = place("hl", [P, 2, UF, SLOTS], F32R, e1 + 4 * 2 * UF * SLOTS)
    tl = place("tl", [P, NT, D], F32R, e3)
    th = place("th", [P, NT, D], F32R, e3 + TD)
    eoT = place("eoT", [P, DC, NT, 2, C], F32, e3)
    GB = 4
    ch = place("ch", [PS, GB, D], F32R, e3 + 8 * DC * SLOTS)
    cl = place("cl", [PS, GB, D], F32R, e3 + 8 * DC * SLOTS + 4 * GB * D)
    dg = place("dg", [P, NT, E, C], F32, e3 + 2 * TD - 4 * NT * E * C)
    assert 8 * DC * SLOTS + 8 * GB * D <= 2 * TD and 16 * UF * SLOTS <= 2 * TD
    dsp = new("dsp", [P, NT, E, C], F32R)
    dpt = new("dpt", [PS, PAIRS, NT, P], F32R)
    xeh, xel = (new(n, [P, DC, E, SLOTS], F32R) for n in ("xeh", "xel"))
    raw_i = new("raw_i", [P, 2, DC, UF * P])
    raw_o = new("raw_o", [P, 2, UF, D])
    wih, wil = (new(n, [P, 2, DC, UF * P], F32R) for n in ("wih", "wil"))
    woh, wol = (new(n, [P, 2, UF, D], F32R) for n in ("woh", "wol"))
    end, at[0] = at[0], at[0] - 8 * UF * D
    lg, ex, pr, mk1, mk2, cm1, cm2, pos = (
        new(n, [P, NT, E]) for n in ("lg", "ex", "pr", "mk1", "mk2", "cm1", "cm2", "pos"))
    top8 = new("top8", [P, NT, 8])
    idx8 = new("idx8", [P, NT, 8], U32)
    idxf = new("idxf", [P, NT, 2])
    lmax, lsum, lrec = (new(n, [P, NT]) for n in ("lmax", "lsum", "lrec"))
    assert at[0] <= end and max(top, end) <= nc.sbuf_usable_end

    ctx = ExitStack()
    with ctx:
        ps = ctx.enter_context(nc.psum_tensor("ps", [P, 8 * BANK], F32))

        def bank(i, n=BANK):
            return ps[:, i * BANK:i * BANK + n]

        def sem(name):
            return ctx.enter_context(nc.semaphore(name))

        def wait(eng, s, value):
            if not isinstance(value, int) or value > 0:
                eng.wait_ge(s, value)

        XT = 2
        x_in = [sem(f"x_in{n}") for n in range(NT // XT)]
        first_in, later_in, wpj_in = sem("first_in"), sem("later_in"), sem("wpj_in")
        wqk_in, wv_in, w_hi, w_lo, wp_hi, wp_lo = (sem(n) for n in ("wqk_in", "wv_in", "w_hi", "w_lo", "wp_hi", "wp_lo"))
        raw_i_in = [sem("raw_i_in0"), sem("raw_i_in1")]
        raw_o_in = [sem("raw_o_in0"), sem("raw_o_in1")]
        ln_step, ln_var, ln_std = sem("ln_step"), sem("ln_var"), sem("ln_std")
        shift_ready, xn_dve, xn_act = sem("shift_ready"), sem("xn_dve"), sem("xn_act")
        ones_set, bd_zero, rp_turned, bd_ready = (sem(n) for n in ("ones_set", "bd_zero", "rp_turned", "bd_ready"))
        xb_ready, k_rows, rows_set = sem("xb_ready"), sem("k_rows"), sem("rows_set")
        rows_in = [sem("rows_in1"), sem("rows_in2")]
        turned, turn_act, turn_dve = sem("turned"), sem("turn_act"), sem("turn_dve")
        proj_mm, q_act, hi_act, lo_dve, v_mm, v_dve = (
            sem(n) for n in ("proj_mm", "q_act", "hi_act", "lo_dve", "v_mm", "v_dve"))
        rel_products_mm, rel_copied, rel_mm, rel_act, rel_dve = (
            sem(n) for n in ("rel_products_mm", "rel_copied", "rel_mm", "rel_act", "rel_dve"))
        heads_in = [sem(f"heads_in{b}") for b in range(3)]
        vh_ready, max_mm, max_red, max_whole, max_turned, mneg_ready, mrow_in = (
            sem(n) for n in ("vh_ready", "max_mm", "max_red", "max_whole", "max_turned", "mneg_ready", "mrow_in"))
        s_mm, exp_done, pv_mm, o_copied, o_turned, o_rec, o_normed = (
            sem(n) for n in ("s_mm", "exp_done", "pv_mm", "o_copied", "o_turned", "o_rec", "o_normed"))
        wproj_mm, x1_ready = sem("wproj_mm"), sem("x1_ready")
        th_ready, tl_ready, logits_mm, rt_step, ex_ready, masks_ready, count_mm = (
            sem(n) for n in ("th_ready", "tl_ready", "logits_mm", "rt_step", "ex_ready", "masks_ready", "count_mm"))
        dsp_ready, dg_ready, gsl_ready = (
            sem(n) for n in ("dsp_ready", "dg_ready", "gsl_ready"))
        dpt_mm, xe_mm, xe_act, xe_dve = (
            sem(n) for n in ("dpt_mm", "xe_mm", "xe_act", "xe_dve"))
        wi_hi, wi_lo, wo_hi, wo_lo = (sem(n) for n in ("wi_hi", "wi_lo", "wo_hi", "wo_lo"))
        h_mm, h_hi, h_lo, y_mm, eo_ready, eo_last = (
            sem(n) for n in ("h_mm", "h_hi", "h_lo", "y_mm", "eo_ready", "eo_last"))
        pair_set, c_turned, c_hi, c_lo, c_mm, c_added, out_done = (
            sem(n) for n in ("pair_set", "c_turned", "c_hi", "c_lo", "c_mm", "c_added", "out_done"))

        block = ctx.enter_context(nc.Block())

        FIRST = [
            (ident[:, :], ident_c), (flip[:, :], flip_c),
            (rp[:, 0, :, :], rel_pos_h.unsqueeze(1).broadcast_to([NREL, HPG, HD])),
            (rp[:, 1, :, :], rel_pos_w.unsqueeze(1).broadcast_to([NREL, HPG, HD])),
            (b6[:, :], b_qkv[0:2 * D].rearrange("(m p) -> m p", p=P)), (onehot[2 * SIDE:4 * SIDE, :], onehot_c),
        ]
        LATER = [
            (bv[:, :], b_qkv[2 * D:3 * D].partition_broadcast(P)), (bpj[:, :], b_proj.partition_broadcast(P)),
            (tri[:, :], tri_c), (slot1[:, :], slot_c), (wrt[:, :, :], w_router.rearrange("(c p) e -> p c e", p=P)),
        ]
        HALF = NT // 2
        HEAD_IN = 16 * 6
        QK = [(kk, c, half) for c in range(DC) for kk in range(2) for half in range(2)]
        QK_BANKS = [6, 7, 4, 5]
        REL = [(kind, c, half) for c in range(DC) for kind in range(2) for half in range(2)]
        V_BANKS = [0, 1, 2, 6]
        X_TURNS, ATTN_TURNS = [0, 1, 2, 3, 4, 5], [0, 3, 1, 4, 2, 5]
        PROJ_BANKS = [6, 7, 0, 1, 3, 4, 5, 6]
        TURN_BANKS, SUM_BANKS, AHEAD = [6, 0, 1, 2], [7, 3, 4, 5], 3

        def dispatched(n):
            return n % 2 * 4, n % DC, n // DC * XT

        def expert_input(n, part):
            b, c, g = dispatched(n)
            src = ps[:, (b + 2 * part) * BANK:(b + 2 * part + 2) * BANK].rearrange("p (g n) -> p g n", g=XT)
            return ((xeh, xel)[part][:, c, :, g * C:(g + XT) * C].rearrange("p e (g s) -> p e g s", g=XT),
                    src[:, :, 0:E * C].rearrange("p g (e s) -> p e g s", e=E))

        def weights(i):
            if i == 2 * DC:
                return wv[:, :, :], wvh[:, :, :], wvl[:, :, :]
            m = (i % 2) * DC + i // 2
            return tuple(w[:, :, m * P:(m + 1) * P] for w in (wqk, wqkh, wqkl))

        def rel_views(part, n):
            kind, c, half = REL[n]
            b, w = bank(2 + n % 2), SIDE // 2
            if kind == 0:
                return rel[0][:, part, c, half * BANK:(half + 1) * BANK], b
            return (rel[1][:, part, c, :].rearrange("p (r w) -> p w r", w=SIDE)[:, half * w:(half + 1) * w, :],
                    b.rearrange("p (w r) -> p w r", w=w))

        @block.sync
        def _(sp):
            for n in range(NT // XT):
                sp.dma_start(xs[:, n * XT:(n + 1) * XT, :], x_v[:, n * XT:(n + 1) * XT, :]).then_inc(x_in[n], 16)
            for dst, src in FIRST:
                sp.dma_start(dst, src).then_inc(first_in, 16)
            for dst, cols, arrived in ((wqk, slice(0, 2 * D), wqk_in), (wv, slice(2 * D, 3 * D), wv_in)):
                sp.dma_start(dst[:, :, :], w_qkv.rearrange("(c p) n -> p c n", p=P)[:, :, cols]).then_inc(arrived, 16)
            for dst, src in LATER:
                sp.dma_start(dst, src).then_inc(later_in, 16)

            def gather_head(h):
                chunk, rows, b = h // HPG, slice(HD * (h % HPG), HD * (h % HPG + 1)), h % 3
                for made in (hi_act, lo_dve, rel_act, rel_dve):
                    sp.wait_ge(made, 4 * (chunk + 1))
                if h == 1:
                    sp.wait_ge(proj_mm, 4 * DC)
                if h == 2:
                    sp.wait_ge(v_mm, NT)
                if h in (1, 2):
                    sp.wait_ge(rows_set, 2)
                    sp.wait_ge(k_rows, 1)
                    for const, part in ((slice(2 * HD, 4 * HD), slice(0, 2)), (slice(HD, 2 * HD), slice(1, 2))):
                        sp.dma_start(kst[h][const, part, :].bitcast(F32), kst[0][const, part, :].bitcast(F32)).then_inc(rows_in[h - 1], 16)
                if h > 2:
                    sp.wait_ge(s_mm, 8 * (h - 2))
                both = [HD, 2, T]
                parts = [(qst[b][0:HD, :, :], qh[rows, chunk, :].unsqueeze(1).broadcast_to(both)),
                         (qst[b][HD:2 * HD, 0, :], ql[rows, chunk, :]),
                         (qst[b][2 * HD:3 * HD, :, :], rel[0][rows, :, chunk, :]),
                         (qst[b][3 * HD:4 * HD, :, :], rel[1][rows, :, chunk, :]),
                         (kst[b][0:HD, :, :], kp[rows, :, chunk, :]),
                         (kst[b][HD:2 * HD, 0, :], kp[rows, 0, chunk, :])]
                for dst, src in parts:
                    sp.dma_start(dst.bitcast(F32), src.bitcast(F32)).then_inc(heads_in[b], 16)

            def max_row(h):
                sp.wait_ge(mneg_ready, h + 1)
                sp.dma_start(qst[h % 3][HD:HD + 1, 1, :].rearrange("o (t q) -> o t q", q=P).bitcast(F32),
                             mneg[:, :].bitcast(F32)).then_inc(mrow_in, 16)

            gather_head(0)
            gather_head(1)
            for h in range(NH):
                max_row(h)
                if h + 2 < NH:
                    gather_head(h + 2)
                if h == NH - 2:
                    sp.wait_ge(s_mm, 8 * (NH - 2))
                    sp.dma_start(wpj[:, :, :], w_proj.rearrange("(c p) n -> p c n", p=P)).then_inc(wpj_in, 16)

            sp.wait_ge(s_mm, 8 * NH)
            for n in range(NT // XT):
                sp.dma_start(xs[:, n * XT:(n + 1) * XT, :], x_v[:, n * XT:(n + 1) * XT, :]).then_inc(x_in[n], 16)

            def load_unit(e, s, u):
                b = s % 2
                wait(sp, wi_lo, u - 1)
                sp.wait_ge(x1_ready, NT)
                sp.dma_start(raw_i[:, b, :, :], wi_v[e, s]).then_inc(raw_i_in[b], 16)
                wait(sp, wo_lo, u - 1)
                sp.wait_ge(x1_ready, NT)
                sp.dma_start(raw_o[:, b, :, :], wo_v[e, s]).then_inc(raw_o_in[b], 16)

            for u in range(PU):
                load_unit(u // UNITS, u % UNITS, u)
            with sp.Fori(0, PAIRS - 1) as pr:
                for k in range(2):
                    for s in range(UNITS):
                        load_unit(2 * pr + 2 + k, s, PU * pr + PU + UNITS * k + s)

            for t in range(NT):
                sp.wait_ge(c_added, NT * (PAIRS - 1) + t + 1)
                sp.dma_start(out_v[:, t, :], xs[:, t, :]).then_inc(out_done, 16)
            sp.wait_ge(out_done, 16 * NT)

        @block.gpsimd
        def _(pool):
            nc.gpsimd.memset(ones[:, :], 1.0).then_inc(ones_set, 1)
            for b in range(2):
                nc.gpsimd.memset(vh[b][:, :, HD:2 * HD], 1.0).then_inc(ones_set, 1)
            pool.wait_ge(wqk_in, 16)
            for i in range(2 * DC + 1):
                if i == 2 * DC:
                    pool.wait_ge(wv_in, 16)
                raw, high, _ = weights(i)
                nc.gpsimd.tensor_copy(high, raw).then_inc(w_hi, 1)

            pool.wait_ge(w_hi, 2 * DC + 1)
            pool.wait_ge(first_in, 16 * len(FIRST))
            nc.gpsimd.memset(qst[0][HD:2 * HD, 1, :].bitcast(F32), 0.0).then_inc(rows_set, 1)
            nc.gpsimd.memset(kst[0][HD:2 * HD, 1, :].bitcast(F32), 1.0).then_inc(rows_set, 1)
            pool.wait_ge(rows_set, 2)
            nc.gpsimd.tensor_copy(kst[0][2 * SIDE:4 * SIDE, :, :],
                                  onehot[2 * SIDE:4 * SIDE, :].unsqueeze(1).broadcast_to([2 * SIDE, 2, T])).then_inc(k_rows, 1)
            pool.wait_ge(k_rows, 1)
            pool.wait_ge(rp_turned, 3)
            nc.gpsimd.memset(vh[2][:, :, HD:2 * HD], 1.0).then_inc(ones_set, 1)
            pool.wait_ge(ones_set, 4)
            pool.wait_ge(proj_mm, 4 * DC)
            nc.gpsimd.memset(qst[1][HD:2 * HD, 1, :].bitcast(F32), 0.0).then_inc(rows_set, 1)
            pool.wait_ge(rows_set, 3)
            pool.wait_ge(v_dve, NT)

            def head_values(h, b):
                wait(pool, pv_mm, 8 * (h - 2))
                nc.gpsimd.tensor_copy(vh[b][:, :, 0:HD], vt[:, :, bass.ts(h, HD)]).then_inc(vh_ready, 1)

            head_values(0, 0)
            pool.wait_ge(vh_ready, 1)
            nc.gpsimd.memset(qst[2][HD:2 * HD, 1, :].bitcast(F32), 0.0).then_inc(rows_set, 1)
            pool.wait_ge(rows_set, 4)
            head_values(1, 1)
            head_values(2, 2)
            with pool.Fori(1, NH // 3) as i:
                for b in range(3):
                    head_values(3 * i + b, b)

            pool.wait_ge(wpj_in, 16)
            nc.gpsimd.tensor_copy(wph[:, :, :], wpj[:, :, :]).then_inc(wp_hi, 1)
            for t in range(NT):
                pool.wait_ge(x_in[t // XT], 32)
                nc.gpsimd.tensor_tensor(xs[:, t, :], xs[:, t, :], bpj[:, :], ALU.add).then_inc(xb_ready, 1)

            def set_pair(pr):
                wait(pool, c_mm, NT * pr)
                wait(pool, c_lo, NT * pr)
                nc.gpsimd.tensor_copy(dpc[:, :, :], dpt[:, pr, :, :].bitcast(F32)).then_inc(pair_set, 1)
                nc.gpsimd.tensor_copy(gsc[:, :], gsl[:, bass.ts(pr, NT)]).then_inc(pair_set, 1)

            pool.wait_ge(gsl_ready, NT)
            set_pair(0)
            with pool.Fori(1, PAIRS) as pr:
                set_pair(pr)

        @block.tensor
        def _(pe):
            mm = nc.tensor.matmul

            pe.wait_ge(first_in, 16 * len(FIRST))
            for kind in range(2):
                nc.tensor.transpose(bank(6)[:, NREL * kind:NREL * (kind + 1)],
                                    rp[:, kind, :, :].rearrange("p a b -> p (a b)"), flip[:, :]).then_inc(rp_turned, 1)
            nc.tensor.transpose(bank(6)[:, 2 * NREL:2 * NREL + 2 * DC], b6[:, :],
                                ident[0:2 * DC, 0:2 * DC]).then_inc(rp_turned, 1)

            def turn(src, banks):
                for k in banks:
                    for t in range(HALF):
                        last = nc.tensor.transpose(bank(k)[:, t * P:(t + 1) * P],
                                                   src[:, k // DC * HALF + t, k % DC * P:(k % DC + 1) * P], ident[:, :])
                    last.then_inc(turned, 1)

            for half in range(2):
                pe.wait_ge(xn_dve, HALF // 2 * (half + 1))
                pe.wait_ge(xn_act, HALF // 2 * (half + 1))
                turn(xn, X_TURNS[DC * half:DC * (half + 1)])

            pe.wait_ge(bd_ready, 2)

            def three(out_bank, stationary, moving, first=True, last=True):
                (sh, sl), (mh, ml) = stationary, moving
                for n, (a, b) in enumerate([(sh, mh), (sh, ml), (sl, mh)]):
                    done = mm(out_bank, a, b, start=first and n == 0, stop=last and n == 2)
                return done

            def qk(n):
                kk, chunk, half = QK[n]
                if half == 0:
                    pe.wait_ge(w_lo, n // 2 + 1)
                if n < 2:
                    pe.wait_ge(turn_dve, DC * (n + 1))
                if n >= 4:
                    was = QK[n - 4]
                    if was[0]:
                        pe.wait_ge(lo_dve, n - 3)
                    else:
                        pe.wait_ge(q_act, 2 * was[1] + was[2] + 1)
                m = kk * DC + chunk
                for c in range(DC):
                    last = three(bank(QK_BANKS[n % 4]), [w[:, c, m * P:(m + 1) * P] for w in (wqkh, wqkl)],
                                 [x_[:, c, half * BANK:(half + 1) * BANK] for x_ in (xnh, xnl)], c == 0, c == DC - 1)
                last.then_inc(proj_mm, 1)

            def rel_products(n):
                kind, c, half = REL[n]
                wait(pe, rel_copied, n - 1)
                for t in range(HALF):
                    for j in range(HPG):
                        r = (half * HALF + t) * HPG + j
                        q_of_r = qf[:, c, r * SIDE:(r + 1) * SIDE] if kind == 0 else qf[:, c, r:T:SIDE]
                        last = mm(bank(n % 2)[j * SIDE:(j + 1) * SIDE, t * P:(t + 1) * P], q_of_r,
                                  bd[:, kind, :, SIDE - 1 - r:2 * SIDE - 1 - r], start=True, stop=True)
                last.then_inc(rel_products_mm, 1)

            def rel_turn(n):
                pe.wait_ge(rel_copied, n + 1)
                wait(pe, rel_dve, n - 1)
                for t in range(HALF):
                    last = nc.tensor.transpose(bank(2 + n % 2)[:, t * P:(t + 1) * P],
                                               rst[:, n % 2, t * P:(t + 1) * P], ident[:, :])
                last.then_inc(rel_mm, 1)

            def rel_terms(first, end, between):
                pe.wait_ge(q_act, end // 2)
                for n in range(first, end):
                    rel_products(n)
                    if n > first:
                        rel_turn(n - 1)
                    between(n)
                rel_turn(end - 1)

            for n in range(4):
                qk(n)
            rel_terms(0, 4, lambda n: None)
            for n in range(4, 4 * DC):
                qk(n)

            def value_tile(t):
                wait(pe, v_dve, t - 3)
                if t == 2:
                    pe.wait_ge(rel_dve, 4 * DC)
                for c in range(DC):
                    last = three(bank(V_BANKS[t % 4], D), [x_[:, c, t * P:(t + 1) * P] for x_ in (xnh, xnl)],
                                 [w[:, c, :] for w in (wvh, wvl)], c == 0, c == DC - 1)
                last.then_inc(v_mm, 1)

            NP = 2 * NT

            def max_scores(h, n, b, p):
                if p == 0:
                    pe.wait_ge(heads_in[b], HEAD_IN * (n + 1))
                wait(pe, max_red, NP * h + p - 1)
                t, half = p // 2, p % 2
                mm(bank(4 + half), qst[b][:, 0, t * P:(t + 1) * P], kst[b][:, 0, half * BANK:(half + 1) * BANK],
                   start=True, stop=True).then_inc(max_mm, 1)

            def turn_max(h):
                pe.wait_ge(max_whole, h + 1)
                wait(pe, o_normed, h - 1)
                nc.tensor.transpose(bank(7)[0:NT, 0:P], rmax[:, :], ident[:, :]).then_inc(max_turned, 1)

            def scores(h, b, t):
                if t == 0:
                    pe.wait_ge(mrow_in, 16 * (h + 1))
                wait(pe, exp_done, 8 * h + t - 1)
                for half in range(2):
                    for part in range(2):
                        last = mm(bank(2 * (t % 2) + half), kst[b][:, part, t * P:(t + 1) * P],
                                  qst[b][:, part, half * BANK:(half + 1) * BANK], start=part == 0, stop=part == 1)
                last.then_inc(s_mm, 1)

            def values(h, b, t):
                pe.wait_ge(exp_done, 8 * h + t + 1)
                if t == 0:
                    pe.wait_ge(vh_ready, h + 1)
                    wait(pe, o_copied, h)
                for half in range(2):
                    last = mm(bank(6)[2 * HD * half:2 * HD * (half + 1), :], vh[b][:, t, :],
                              prob[:, t % 2, half * BANK:(half + 1) * BANK], start=t == 0, stop=t == NT - 1)
                last.then_inc(pv_mm, 1)

            def turn_output(h):
                pe.wait_ge(o_copied, h + 1)
                for j in range(HALF):
                    last = nc.tensor.transpose(bank(7)[:, j * P:(j + 1) * P], osb[:, j * P:(j + 1) * P], ident[:, :])
                last.then_inc(o_turned, 1)

            PIECES = [(0, 3), (3, 6), (6, 9), (9, 12), (12, 15), (15, 16), (16, 16), (16, 16)]

            def head(h, n, b, first=False, last=False):
                nxt = (n + b // 2, (b + 1) % 3)
                for t in range(NT):
                    pieces = [] if last else list(range(*PIECES[t]))
                    if t == 6 and not last:
                        turn_max(h + 1)
                    if t == 2 and not first:
                        wait(pe, mneg_ready, h + 1)
                        turn_output(h - 1)
                    for p in pieces[:1]:
                        max_scores(h + 1, *nxt, p)
                    if t == 1 and first:
                        pe.wait_ge(v_dve, NT)
                    scores(h, b, t)
                    for p in pieces[1:2]:
                        max_scores(h + 1, *nxt, p)
                    if t > 0:
                        values(h, b, t - 1)
                    elif not first:
                        values(h - 1, (b - 1) % 3, NT - 1)
                    for p in pieces[2:]:
                        max_scores(h + 1, *nxt, p)

            def first_max(n):
                if n == 4:
                    pe.wait_ge(lo_dve, 4 * DC)
                    pe.wait_ge(rows_set, 2)
                    pe.wait_ge(k_rows, 1)
                for p in range(2 * (n - 4), 2 * (n - 3)):
                    max_scores(0, 0, 0, p)

            rel_terms(4, 4 * DC, first_max)
            pe.wait_ge(w_lo, 2 * DC + 1)
            for t in range(NT):
                value_tile(t)
                if t == 1:
                    turn_max(0)
            pe.wait_ge(v_dve, NT - 2)
            pe.wait_ge(rows_set, 3)
            pe.wait_ge(rows_in[0], 32)
            head(0, 0, 0, first=True)
            pe.wait_ge(rows_set, 4)
            pe.wait_ge(rows_in[1], 32)
            with pe.Fori(0, (NH - 3) // 3) as i:
                for j in range(1, 4):
                    head(3 * i + j, i + j // 3, j % 3)
            head(NH - 2, (NH - 2) // 3, (NH - 2) % 3)
            head(NH - 1, (NH - 1) // 3, (NH - 1) % 3, last=True)
            values(NH - 1, (NH - 1) % 3, NT - 1)
            turn(attn, ATTN_TURNS[0:2])
            pe.wait_ge(o_normed, NH - 1)
            turn_output(NH - 1)
            turn(attn, ATTN_TURNS[2:4])
            pe.wait_ge(o_normed, NH)
            turn(attn, ATTN_TURNS[4:6])

            pe.wait_ge(later_in, 16 * len(LATER))
            pe.wait_ge(wp_lo, 1)
            for t in range(NT):
                if t in (0, HALF):
                    pe.wait_ge(turn_dve, 4 * DC - (1 if t == 0 else 0))
                if t == NT - 1:
                    pe.wait_ge(x1_ready, 1)
                for c in range(DC):
                    last = three(bank(PROJ_BANKS[t], D), [x_[:, c, t * P:(t + 1) * P] for x_ in (ath, atl)],
                                 [w[:, c, :] for w in (wph, wpl)], c == 0, c == DC - 1)
                last.then_inc(wproj_mm, 1)

            for half in range(2):
                pe.wait_ge(xn_dve, HALF // 2 * (half + 3))
                pe.wait_ge(xn_act, HALF // 2 * (half + 3))
                turn(tn, X_TURNS[DC * half:DC * (half + 1)])
                pe.wait_ge(turn_act, 4 * DC + (3, 5)[half])
                pe.wait_ge(turn_dve, 4 * DC + half)
                for g in range(half * HALF, (half + 1) * HALF):
                    for c in range(DC):
                        last = mm(bank(7)[:, g * E:(g + 1) * E], tnT[:, c, g * P:(g + 1) * P], wrt[:, c, :],
                                  start=c == 0, stop=c == DC - 1)
            last.then_inc(logits_mm, 1)
            pe.wait_ge(masks_ready, 2)
            first_choice = mk1[:, :, :].rearrange("p g e -> p (g e)")
            second_choice = mk2[:, :, :].rearrange("p g e -> p (g e)")
            W = NT * E
            mm(bank(6, W), tri[:, :], first_choice, start=True, stop=True).then_inc(count_mm, 1)
            mm(bank(5, W), tri[:, :], second_choice, start=True, stop=False)
            mm(bank(5, W), ones[:, :], first_choice, start=False, stop=True).then_inc(count_mm, 1)

            pe.wait_ge(th_ready, NT)
            pe.wait_ge(tl_ready, NT)
            STEPS = DC * NT // XT
            for n in range(STEPS):
                b, c, first_g = dispatched(n)
                pe.wait_ge(dsp_ready, n // DC + 1)
                for part, (x_, left) in enumerate(((th, xe_act), (tl, xe_dve))):
                    wait(pe, left, n - 1)
                    for g in range(first_g, first_g + XT):
                        last = mm(bank(b + 2 * part + g - first_g, E * C), x_[:, g, c * P:(c + 1) * P],
                                  dsp[:, g, :, :].rearrange("p e c -> p (e c)"), start=True, stop=True)
                    last.then_inc(xe_mm, 1)
            pe.wait_ge(xe_act, STEPS)
            pe.wait_ge(xe_dve, STEPS)

            def slot_side(n):
                if n == 0:
                    pe.wait_ge(dg_ready, 1)
                wait(pe, gsl_ready, n - 1)
                pr, half = n // 2, n % 2
                for q in range(HALF):
                    last = nc.tensor.transpose(
                        bank(6 + half)[0:PS, q * P:(q + 1) * P],
                        dg[:, half * HALF + q, 2 * pr:2 * pr + 2, :].rearrange("p e c -> p (e c)"), ident[:, :])
                last.then_inc(dpt_mm, 1)

            def hidden(e, b, v, between):
                pe.wait_ge(wi_hi, v + 1)
                pe.wait_ge(wi_lo, v + 1)
                for k in range(UF):
                    wait(pe, h_lo, UF * (v - 1) + k + 1)
                    terms = [(wih, xeh), (wih, xel), (wil, xeh)]
                    for c in range(DC):
                        for n, (w, xe) in enumerate(terms):
                            last = mm(bank(k, SLOTS), w[:, b, c, k * P:(k + 1) * P], xe[:, c, e, :],
                                      start=c == 0 and n == 0, stop=c == DC - 1 and n == 2)
                    last.then_inc(h_mm, 1)
                    between(k)

            def output(s, e, v, between):
                b = s % 2
                pe.wait_ge(wo_hi, v + 1)
                pe.wait_ge(wo_lo, v + 1)
                if s == 0:
                    wait(pe, eo_ready, DC * e)
                for k in range(UF):
                    pe.wait_ge(h_lo, UF * v + k + 1)
                    for c in range(DC):
                        for n, (w, h) in enumerate([(woh, hh), (woh, hl), (wol, hh)]):
                            last = mm(bank(3 + c, SLOTS), w[:, b, k, c * P:(c + 1) * P], h[:, b, k, :],
                                      start=s == 0 and k == 0 and n == 0,
                                      stop=s == UNITS - 1 and k == UF - 1 and n == 2)
                    if k == UF - 1:
                        last.then_inc(y_mm, 1)
                    between(k)

            def combine_turn(g, turn_bank):
                for c in range(DC):
                    last = nc.tensor.transpose(bank(turn_bank)[0:PS, c * P:(c + 1) * P],
                                               eoT[:, c, g, :, :].rearrange("p e s -> p (e s)"), ident[:, :])
                last.then_inc(c_turned, 1)

            def combine_sum(pr, g, sum_bank):
                pe.wait_ge(c_lo, NT * pr + g + 1)
                mm(bank(sum_bank, D), dpc[:, g, :], ch[:, g % GB, :], start=True, stop=False)
                mm(bank(sum_bank, D), dpc[:, g, :], cl[:, g % GB, :], start=False, stop=True).then_inc(c_mm, 1)

            def combine_between(pr, g):
                if g == 0:
                    pe.wait_ge(eo_ready, DC * (2 * pr + 2))
                    pe.wait_ge(pair_set, 2 * pr + 2)
                else:
                    pe.wait_ge(c_lo, NT * pr + g)
                    wait(pe, c_added, NT * pr + g - 1)
                if g < NT:
                    combine_turn(g, 6)
                if g > 0:
                    combine_sum(pr, g - 1, 7)

            def nothing(k):
                pass

            def pair(pr, first=False, last=False):
                for k in range(PU):
                    v = PU * pr + k

                    def between(j):
                        if k in (1, 2, 3) and j % 2 == 1:
                            n = UF * (k - 1) + j // 2
                            if not first:
                                combine_between(pr - 1, n)
                            elif n < NT:
                                slot_side(n)

                    if not (last and k == PU - 1):
                        hidden(2 * pr + (k + 1) // UNITS, (k + 1) % 2, v + 1, between)
                    output(k % UNITS, 2 * pr + k // UNITS, v, lambda j: between(UF + j))

            hidden(0, 0, 0, nothing)
            pair(0, first=True)
            with pe.Fori(1, PAIRS - 1) as pr:
                pair(pr)
            pair(PAIRS - 1, last=True)
            pe.wait_ge(eo_ready, DC * E - 1)
            pe.wait_ge(eo_last, 1)
            pe.wait_ge(pair_set, 2 * PAIRS)
            done = NT * (PAIRS - 1)
            for g in range(AHEAD):
                combine_turn(g, TURN_BANKS[g])
            for g in range(NT):
                if g >= 4:
                    pe.wait_ge(c_added, done + g - 3)
                combine_sum(PAIRS - 1, g, SUM_BANKS[g % 4])
                if g + AHEAD < NT:
                    combine_turn(g + AHEAD, TURN_BANKS[(g + AHEAD) % 4])

        @block.scalar
        def _(act):
            run = nc.scalar.activation

            def turn_back(dst, n, banks):
                for i, k in enumerate(banks):
                    act.wait_ge(turned, 2 * DC * n + i + 1)
                    run(dst[:, k % DC, (k // DC) * BANK:(k // DC + 1) * BANK], bank(k), ACT.Copy).then_inc(turn_act, 1)

            def norm(src, dst, n):
                act.wait_ge(ln_var, n + 1)
                run(std[:, 0:HALF], veps[:, 0:HALF], ACT.Sqrt).then_inc(ln_std, 1)
                act.wait_ge(shift_ready, n + 1)
                for j in range(1, HALF, 2):
                    t = n % 2 * HALF + j
                    run(dst[:, t, :], src[:, t, :], ACT.Identity, scale=rstd[:, j:j + 1], bias=mv[:, t, 1:2]).then_inc(xn_act, 1)

            norm(xs, xn, 0)
            norm(xs, xn, 1)
            turn_back(xnh, 0, X_TURNS)
            act.wait_ge(bd_ready, 2)

            def units(first, end):
                for n in range(first, end):
                    kk, c, half = QK[n]
                    cols = slice(half * BANK, (half + 1) * BANK)
                    act.wait_ge(proj_mm, n + 1)
                    if kk:
                        run(kp[:, 0, c, cols], bank(QK_BANKS[n % 4]), ACT.Identity, bias=bqk[:, DC + c:DC + c + 1]).then_inc(hi_act, 1)
                    else:
                        run(qf[:, c, cols], bank(QK_BANKS[n % 4]), ACT.Identity, bias=bqk[:, c:c + 1]).then_inc(q_act, 1)
                        act.wait_ge(q_act, 2 * c + half + 1)
                        run(qh[:, c, cols], qf[:, c, cols], ACT.Copy, scale=SCALE).then_inc(hi_act, 1)

            def rel_high(n):
                act.wait_ge(rel_mm, n + 1)
                dst, src = rel_views(0, n)
                run(dst, src, ACT.Copy).then_inc(rel_act, 1)

            def rels(first, end):
                for n in range(first, end):
                    act.wait_ge(rel_products_mm, n + 1)
                    wait(act, rel_mm, n - 1)
                    run(rst[:, n % 2, :], bank(n % 2), ACT.Copy).then_inc(rel_copied, 1)
                    if n > first:
                        rel_high(n - 1)
                rel_high(end - 1)

            units(0, 4)
            rels(0, 4)
            units(4, 4 * DC)
            rels(4, 4 * DC)

            def exps(h, first=False):
                for t in range(NT):
                    act.wait_ge(s_mm, 8 * h + t + 1)
                    wait(act, pv_mm, 8 * h + t - 1)
                    run(prob[:, t % 2, :], ps[:, 2 * (t % 2) * BANK:2 * (t % 2 + 1) * BANK], ACT.Exp).then_inc(exp_done, 1)
                    if t == 0 and not first:
                        copy_output(h - 1)

            def copy_output(h):
                act.wait_ge(pv_mm, 8 * h + 8)
                run(osb[:, :], bank(6), ACT.Copy).then_inc(o_copied, 1)

            exps(0, first=True)
            with act.Fori(1, NH) as h:
                exps(h)
            copy_output(NH - 1)
            turn_back(ath, 1, ATTN_TURNS)

            def split_wi(b, v, n):
                act.wait_ge(raw_i_in[b], 16 * (n + 1))
                wait(act, h_mm, UF * (v - 1))
                run(wih[:, b, :, :], raw_i[:, b, :, :], ACT.Copy).then_inc(wi_hi, 1)

            def split_wo(b, v, n):
                act.wait_ge(raw_o_in[b], 16 * (n + 1))
                wait(act, y_mm, v - 1)
                run(woh[:, b, :, :], raw_o[:, b, :, :], ACT.Copy).then_inc(wo_hi, 1)

            def high(half):
                for t in range(half * HALF, (half + 1) * HALF):
                    act.wait_ge((xn_dve, xn_act)[t % 2], NT // 2 + t // 2 + 1)
                    run(th[:, t, :], tn[:, t, :], ACT.Copy).then_inc(th_ready, 1)

            def tokens_back(banks):
                for k in banks:
                    act.wait_ge(turned, 4 * DC + k + 1)
                    run(tnT[:, k % DC, (k // DC) * BANK:(k // DC + 1) * BANK], bank(k), ACT.Copy).then_inc(turn_act, 1)

            norm(xs, tn, 2)
            high(0)
            tokens_back([0, 1, 2])
            norm(xs, tn, 3)
            high(1)
            split_wi(0, 0, 0)
            tokens_back([3, 5])
            act.wait_ge(rt_step, 2)
            run(ex[:, :, :], lg[:, :, :], ACT.Exp).then_inc(ex_ready, 1)
            split_wi(1, 1, 0)
            split_wo(0, 0, 0)
            for n in range(DC * NT // XT):
                act.wait_ge(xe_mm, 2 * n + 1)
                run(*expert_input(n, 0), ACT.Copy).then_inc(xe_act, 1)

            def relu(b, v, k):
                act.wait_ge(h_mm, UF * v + k + 1)
                run(hh[:, b, k, :], bank(k, SLOTS), ACT.Relu).then_inc(h_hi, 1)

            def leave(pr, k, chunks=range(DC)):
                act.wait_ge(y_mm, UNITS * (2 * pr + k + 1))
                wait(act, c_turned, NT * pr)
                for c in chunks:
                    run(eoT[:, c, :, k, :], bank(3 + c, SLOTS).rearrange("p (g s) -> p g s", s=C), ACT.Copy).then_inc(eo_ready, 1)

            def gated(pr, g, turn_bank=6):
                act.wait_ge(c_turned, NT * pr + g + 1)
                if g == 0:
                    act.wait_ge(pair_set, 2 * pr + 2)
                if g >= GB:
                    act.wait_ge(c_mm, NT * pr + g + 1 - GB)
                run(ch[:, g % GB, :], bank(turn_bank, D)[0:PS, :], ACT.Copy, scale=gsc[:, g:g + 1]).then_inc(c_hi, 1)

            def pair(pr, first=False, last=False):
                for k in range(PU):
                    v = PU * pr + k

                    def step(n):
                        n += UF * (k - 2)
                        if first or k not in (2, 3, 4) or n == NT:
                            return
                        gated(pr - 1, n)

                    wait(act, y_mm, v - 1)
                    relu(k % 2, v, 0)
                    relu(k % 2, v, 1)
                    step(0)
                    relu(k % 2, v, 2)
                    if k == 0 and not first:
                        leave(pr - 1, 1)
                    if not (last and k + 2 >= PU):
                        split_wi(k % 2, v + 2, PU // 2 * pr + k // 2 + 1)
                    step(1)
                    if k == UNITS:
                        leave(pr, 0)
                    step(2)
                    if not (last and k + 1 >= PU):
                        split_wo((k + 1) % 2, v + 1, PU // 2 * pr + (k + 1) // 2)

            pair(0, first=True)
            with act.Fori(1, PAIRS - 1) as pr:
                pair(pr)
            pair(PAIRS - 1, last=True)
            leave(PAIRS - 1, 1, [0, 2])
            for g in range(NT):
                gated(PAIRS - 1, g, TURN_BANKS[g % 4])

        @block.vector
        def _(dve):
            ve = nc.vector
            stt = ve.scalar_tensor_tensor

            ln_steps = [0]

            def ln_next(ins, count=1):
                ln_steps[0] += count
                ins.then_inc(ln_step, count)

            def norm(src, dst, eps, n, ready):
                tiles = range(n % 2 * HALF, (n % 2 + 1) * HALF)
                for t in tiles:
                    ready(t)
                    ln_next(ve.bn_stats(stats[:, t, :], src[:, t, :]))
                dve.wait_ge(ln_step, ln_steps[0])
                for t in tiles:
                    ln_next(ve.bn_aggr(mv[:, t, :], stats[:, t, :]))
                dve.wait_ge(ln_step, ln_steps[0])
                ve.tensor_scalar(veps[:, 0:HALF], mv[:, n % 2 * HALF:(n % 2 + 1) * HALF, 1], eps, None, ALU.add).then_inc(ln_var, 1)
                dve.wait_ge(ln_std, n + 1)
                ln_next(ve.reciprocal(rstd[:, 0:HALF], std[:, 0:HALF]))
                dve.wait_ge(ln_step, ln_steps[0])
                stt(out=mv[:, tiles[0]:tiles[0] + HALF, 1], in0=mv[:, tiles[0]:tiles[0] + HALF, 0], scalar=-1.0,
                    in1=rstd[:, 0:HALF], op0=ALU.mult, op1=ALU.mult).then_inc(shift_ready, 1)
                for t in tiles[::2]:
                    ve.tensor_scalar(dst[:, t, :], src[:, t, :], mv[:, t, 0:1], rstd[:, t % HALF:t % HALF + 1],
                                     ALU.subtract, ALU.mult).then_inc(xn_dve, 1)

            def turn_back(dst, high, n, banks, first=0):
                for i, k in enumerate(banks):
                    dve.wait_ge(turn_act, 2 * DC * n + first + i + 1)
                    here = (slice(None), k % DC, slice((k // DC) * BANK, (k // DC + 1) * BANK))
                    ve.tensor_tensor(dst[here], bank(k), high[here].bitcast(F32), ALU.subtract).then_inc(turn_dve, 1)

            def weights_low(i):
                dve.wait_ge(w_hi, i + 1)
                raw, high, low = weights(i)
                ve.tensor_tensor(low, raw, high.bitcast(F32), ALU.subtract).then_inc(w_lo, 1)

            ve.memset(bd[:, :, :, :], 0.0).then_inc(bd_zero, 1)
            for half in range(2):
                norm(xs, xn, LN_C_EPS, half, lambda t: dve.wait_ge(x_in[t // XT], 16))
            dve.wait_ge(bd_zero, 1)
            dve.wait_ge(rp_turned, 3)
            ve.tensor_copy(bqk[:, :], bank(6)[:, 2 * NREL:2 * NREL + 2 * DC]).then_inc(bd_ready, 1)
            for j in range(HPG):
                rows = slice(HD * j, HD * (j + 1))
                last = ve.tensor_copy(bd[rows, :, j, :], bank(6, 2 * NREL)[rows, :].rearrange("p (k r) -> p k r", k=2))
            last.then_inc(bd_ready, 1)
            dve.wait_ge(xn_dve, NT // 2)
            dve.wait_ge(xn_act, NT // 2)
            turn_back(xnl, xnh, 0, X_TURNS[0:DC])
            weights_low(0)
            turn_back(xnl, xnh, 0, X_TURNS[DC:2 * DC], DC)
            def units(first, end):
                for n in range(first, end):
                    kk, c, half = QK[n]
                    cols = slice(half * BANK, (half + 1) * BANK)
                    if half == 0:
                        weights_low(n // 2 + 1)
                    dve.wait_ge(hi_act, n + 1)
                    if kk:
                        stt(out=kp[:, 1, c, cols], in0=bank(QK_BANKS[n % 4]), scalar=bqk[:, DC + c:DC + c + 1],
                            in1=kp[:, 0, c, cols].bitcast(F32), op0=ALU.add, op1=ALU.subtract).then_inc(lo_dve, 1)
                    else:
                        stt(out=ql[:, c, cols], in0=qf[:, c, cols], scalar=SCALE, in1=qh[:, c, cols].bitcast(F32),
                            op0=ALU.mult, op1=ALU.subtract).then_inc(lo_dve, 1)

            def rel_low(n):
                dve.wait_ge(rel_act, n + 1)
                dst, src = rel_views(1, n)
                ve.tensor_tensor(dst, src, rel_views(0, n)[0].bitcast(F32), ALU.subtract).then_inc(rel_dve, 1)

            units(0, 4)
            for n in range(4):
                rel_low(n)
            units(4, 4 * DC)

            def reduce_max(h, p):
                dve.wait_ge(max_mm, 2 * NT * h + p + 1)
                ve.tensor_reduce(rhalf[:, p // 2, p % 2:p % 2 + 1], bank(4 + p % 2), AX_X, ALU.max).then_inc(max_red, 1)

            def whole_max(h):
                dve.wait_ge(max_red, 2 * NT * (h + 1))
                ve.tensor_reduce(rmax[:, :], rhalf[:, :, :], AX_X, ALU.max).then_inc(max_whole, 1)

            def negate_max(h):
                dve.wait_ge(max_turned, h + 1)
                wait(dve, mrow_in, 16 * h)
                ve.tensor_scalar(mneg[:, :], bank(7)[0:NT, 0:P], -1.0, None, ALU.mult).then_inc(mneg_ready, 1)

            def normalise(h):
                turned_o = bank(7).rearrange("p (j s c) -> p s j c", s=2, c=2 * HD)
                dve.wait_ge(o_turned, h + 1)
                ve.reciprocal(rl[:, :, :], turned_o[:, :, :, HD]).then_inc(o_rec, 1)
                dve.wait_ge(o_rec, h + 1)
                ve.tensor_tensor(attn[:, :, bass.ts(h, HD)].rearrange("p (s j) d -> p s j d", s=2),
                                 turned_o[:, :, :, 0:HD],
                                 rl[:, :, :].unsqueeze(3).broadcast_to([P, 2, HALF, HD]), ALU.mult).then_inc(o_normed, 1)

            def head(h, first=False):
                for p in range(2 * NT):
                    if p == 6 and not first:
                        normalise(h - 1)
                    reduce_max(h + 1, p)
                whole_max(h + 1)
                negate_max(h + 1)

            for n in range(4, 4 * DC):
                reduce_max(0, 2 * (n - 4))
                reduce_max(0, 2 * (n - 4) + 1)
                rel_low(n)
            whole_max(0)
            for t in range(NT):
                dve.wait_ge(v_mm, t + 1)
                ve.tensor_tensor(vt[:, t, :], bank(V_BANKS[t % 4], D), bv[:, :], ALU.add).then_inc(v_dve, 1)
                if t == 1:
                    negate_max(0)
            head(0, first=True)
            with dve.Fori(1, NH - 1) as h:
                head(h)
            normalise(NH - 2)
            dve.wait_ge(wp_hi, 1)
            ve.tensor_tensor(wpl[:, :, :], wpj[:, :, :], wph[:, :, :].bitcast(F32), ALU.subtract).then_inc(wp_lo, 1)
            turn_back(atl, ath, 1, ATTN_TURNS[0:2])
            normalise(NH - 1)
            turn_back(atl, ath, 1, ATTN_TURNS[2:6], 2)

            dve.wait_ge(xb_ready, NT)

            def residual(t):
                dve.wait_ge(wproj_mm, t + 1)
                ve.tensor_tensor(xs[:, t, :], bank(PROJ_BANKS[t], D), xs[:, t, :], ALU.add).then_inc(x1_ready, 1)
                dve.wait_ge(x1_ready, t + 1)

            def split_wi(b, v):
                dve.wait_ge(wi_hi, v + 1)
                ve.tensor_tensor(wil[:, b, :, :], raw_i[:, b, :, :], wih[:, b, :, :].bitcast(F32),
                                 ALU.subtract).then_inc(wi_lo, 1)

            def split_wo(b, v):
                dve.wait_ge(wo_hi, v + 1)
                ve.tensor_tensor(wol[:, b, :, :], raw_o[:, b, :, :], woh[:, b, :, :].bitcast(F32),
                                 ALU.subtract).then_inc(wo_lo, 1)

            def low(half):
                for t in range(half * HALF, (half + 1) * HALF):
                    dve.wait_ge(th_ready, t + 1)
                    ve.tensor_tensor(tl[:, t, :], tn[:, t, :], th[:, t, :].bitcast(F32), ALU.subtract).then_inc(tl_ready, 1)

            for half in range(2):
                norm(xs, tn, LN_T_EPS, 2 + half, residual)
            low(0)
            split_wi(0, 0)
            dve.wait_ge(turned, 4 * DC + 5)
            ve.tensor_copy(tnT[:, 1, BANK:2 * BANK], bank(4)).then_inc(turn_dve, 1)
            low(1)

            steps = [0]

            def step(ins):
                steps[0] += 1
                ins.then_inc(rt_step, 1)
                dve.wait_ge(rt_step, steps[0])

            def over(v, n):
                return v.unsqueeze(len(v.shape)).broadcast_to([*v.shape, n])

            logits = bank(7, NT * E).rearrange("p (g e) -> p g e", e=E)
            dve.wait_ge(logits_mm, 1)
            step(ve.tensor_reduce(lmax[:, :], logits, AX_X, ALU.max))
            step(ve.tensor_tensor(lg[:, :, :], logits, over(lmax[:, :], E), ALU.subtract))
            dve.wait_ge(ex_ready, 1)
            step(ve.tensor_reduce(lsum[:, :], ex[:, :, :], AX_X, ALU.add))
            step(ve.reciprocal(lrec[:, :], lsum[:, :]))
            step(ve.tensor_tensor(pr[:, :, :], ex[:, :, :], over(lrec[:, :], E), ALU.mult))
            for g in range(NT):
                last = ve.max(top8[:, g, :], pr[:, g, :])
                if g < NT - 1:
                    last.then_inc(rt_step, 1)
                    steps[0] += 1
            step(last)
            for g in range(NT):
                last = ve.max_index(idx8[:, g, :], top8[:, g, :], pr[:, g, :])
                if g < NT - 1:
                    last.then_inc(rt_step, 1)
                    steps[0] += 1
            step(last)
            step(ve.tensor_copy(idxf[:, :, :], idx8[:, :, 0:2]))
            step(ve.tensor_scalar(idxf[:, :, :], idxf[:, :, :], 1.0, None, ALU.add))
            number = slot1[:, 0:E].unsqueeze(1).broadcast_to([P, NT, E])
            ve.tensor_tensor(mk1[:, :, :], number, idxf[:, :, 0:1].broadcast_to([P, NT, E]), ALU.is_equal).then_inc(masks_ready, 1)
            ve.tensor_tensor(mk2[:, :, :], number, idxf[:, :, 1:2].broadcast_to([P, NT, E]), ALU.is_equal).then_inc(masks_ready, 1)
            dve.wait_ge(masks_ready, 2)
            step(ve.tensor_tensor(gate[:, :, :], mk1[:, :, :], top8[:, :, 0:1].broadcast_to([P, NT, E]), ALU.mult))
            step(ve.tensor_tensor(cm1[:, :, :], mk2[:, :, :], top8[:, :, 1:2].broadcast_to([P, NT, E]), ALU.mult))
            step(ve.tensor_tensor(gate[:, :, :], gate[:, :, :], cm1[:, :, :], ALU.add))
            dve.wait_ge(count_mm, 2)
            step(ve.tensor_tensor(cm1[:, :, :], bank(6, NT * E).rearrange("p (g e) -> p g e", e=E), mk1[:, :, :], ALU.mult))
            step(ve.tensor_tensor(cm2[:, :, :], bank(5, NT * E).rearrange("p (g e) -> p g e", e=E), mk2[:, :, :], ALU.mult))
            step(ve.tensor_tensor(pos[:, :, :], cm1[:, :, :], cm2[:, :, :], ALU.add))
            for g in range(0, NT, XT):
                ve.tensor_tensor(dsp[:, g:g + XT, :, :].rearrange("p g e c -> p (g e) c"),
                                 slot1[:, :].unsqueeze(1).broadcast_to([P, XT * E, C]),
                                 over(pos[:, g:g + XT, :].rearrange("p g e -> p (g e)"), C), ALU.is_equal).then_inc(dsp_ready, 1)
            for n in range(DC * NT // XT):
                dve.wait_ge(xe_mm, 2 * n + 2)
                ve.tensor_copy(*expert_input(n, 1)).then_inc(xe_dve, 1)

            def relu_low(b, v, k):
                dve.wait_ge(h_hi, UF * v + k + 1)
                stt(out=hl[:, b, k, :], in0=bank(k, SLOTS), scalar=0.0, in1=hh[:, b, k, :].bitcast(F32),
                    op0=ALU.max, op1=ALU.subtract).then_inc(h_lo, 1)

            def combine(pr, g, turn_bank=6, sum_bank=7):
                if g < NT:
                    dve.wait_ge(c_hi, NT * pr + g + 1)
                    if g >= GB:
                        dve.wait_ge(c_mm, NT * pr + g + 1 - GB)
                    stt(out=cl[:, g % GB, :], in0=bank(turn_bank, D)[0:PS, :], scalar=gsc[:, g:g + 1],
                        in1=ch[:, g % GB, :].bitcast(F32), op0=ALU.mult, op1=ALU.subtract).then_inc(c_lo, 1)
                if g > 0:
                    dve.wait_ge(c_mm, NT * pr + g)
                    ve.tensor_tensor(xs[:, g - 1, :], bank(sum_bank, D), xs[:, g - 1, :], ALU.add).then_inc(c_added, 1)

            def slot_side(n):
                turned_g = bank(6 + n % 2)[0:PS, :]
                groups = slice(n % 2 * HALF, (n % 2 + 1) * HALF)
                dve.wait_ge(dpt_mm, n + 1)
                ve.tensor_scalar(dpt[:, n // 2, groups, :].rearrange("p g s -> p (g s)"), turned_g,
                                 0.0, None, ALU.is_gt)
                ve.tensor_reduce(gsl[:, n * HALF:(n + 1) * HALF], turned_g.rearrange("p (g s) -> p g s", g=HALF),
                                 AX_X, ALU.add).then_inc(gsl_ready, 1)

            def pair(pr, first=False, last=False):
                for k in range(PU):
                    v = PU * pr + k

                    def step(n):
                        n += UF * (k - 2)
                        if k not in (2, 3, 4):
                            return
                        if not first:
                            combine(pr - 1, n)
                        elif n < NT:
                            slot_side(n)

                    relu_low(k % 2, v, 0)
                    relu_low(k % 2, v, 1)
                    step(0)
                    relu_low(k % 2, v, 2)
                    if not (last and k + 2 >= PU):
                        split_wi(k % 2, v + 2)
                    step(1)
                    step(2)
                    if not (last and k + 1 >= PU):
                        split_wo((k + 1) % 2, v + 1)
                    if first and k == 0:
                        ve.tensor_tensor(dg[:, :, :, :].rearrange("p g e c -> p (g e) c"),
                                         dsp[:, :, :, :].rearrange("p g e c -> p (g e) c").bitcast(F32),
                                         over(gate[:, :, :].rearrange("p g e -> p (g e)"), C), ALU.mult).then_inc(dg_ready, 1)

            split_wi(1, 1)
            split_wo(0, 0)
            pair(0, first=True)
            with dve.Fori(1, PAIRS - 1) as q:
                pair(q)
            pair(PAIRS - 1, last=True)
            dve.wait_ge(y_mm, UNITS * E)
            ve.tensor_copy(eoT[:, 1, :, 1, :], bank(4, SLOTS).rearrange("p (g s) -> p g s", s=C)).then_inc(eo_last, 1)
            for g in range(NT + 1):
                combine(PAIRS - 1, g, TURN_BANKS[g % 4], SUM_BANKS[(g - 1) % 4])


_INS = ['x', 'L0_conv_w_qkv', 'L0_conv_b_qkv', 'L0_conv_w_proj', 'L0_conv_b_proj', 'L0_conv_rel_pos_h',
        'L0_conv_rel_pos_w', 'L0_ffn_w_router', 'L0_ffn_wi', 'L0_ffn_wo']


def kernel(**inputs):
    import numpy as _np
    import concourse.bacc as _bacc
    from concourse import mybir as _mybir
    from concourse.bass_utils import run_bass_kernel_spmd as _run

    arrays = {f"in_{n}": _np.ascontiguousarray(inputs[n]) for n in _INS}
    key = _np.arange(SIDE * SIDE)
    arrays["c_ident"] = _np.eye(P, dtype=_np.float32)
    arrays["c_flip"] = _np.eye(2 * SIDE - 1, dtype=_np.float32)[::-1].copy()
    arrays["c_onehot"] = _np.concatenate([
        (key[None, :] // SIDE == _np.arange(SIDE)[:, None]), (key[None, :] % SIDE == _np.arange(SIDE)[:, None]),
    ]).astype(_np.float32)
    arrays["c_before"] = _np.triu(_np.ones((P, P), _np.float32))
    experts = arrays["in_L0_ffn_wi"].shape[0]
    slots = max(int(2 * 1.25 * P / experts), 4)
    arrays["c_slots"] = _np.tile(_np.arange(1, slots + 1, dtype=_np.float32), (P, 1))

    nc = _bacc.Bacc("TRN2", target_bir_lowering=False, num_devices=1)
    args = [nc.dram_tensor(n, a.shape, _mybir.dt.from_np(a.dtype), kind="ExternalInput").ap() for n, a in arrays.items()]
    out = nc.dram_tensor("out_0", arrays["in_x"].shape, F32, kind="ExternalOutput").ap()
    metaformer_layer(nc, *args, out)
    r = _run(nc, [arrays], core_ids=[0])
    return r.results[0]["out_0"]
```
